# Optimizing a Trainium2 kernel written in Bass

```python
import numpy as np
import jax
import jax.numpy as jnp

def _softmax(x, axis=-1):
    return jax.nn.softmax(x, axis=axis)

def _gelu(x):
    return jax.nn.gelu(x, approximate=True)

def _silu(x):
    return jax.nn.silu(x)

def _sigmoid(x):
    return jax.nn.sigmoid(x)

def _layernorm(x, axis=-1, eps=1e-05):
    m = jnp.mean(x, axis=axis, keepdims=True)
    v = jnp.var(x, axis=axis, keepdims=True)
    return (x - m) / jnp.sqrt(v + eps)

def _scatter_add(tgt, idx, src, axis=0):
    return tgt.at[idx].add(src)

def _segment_sum(src, seg, n):
    return jax.ops.segment_sum(src, seg, n)
kernel_name = 'mk_seq_postln_d1_jaxref_r4_5ff36b'

def setup_inputs(seed: int=0):
    np.random.seed(seed)
    _w = jnp.asarray

    def _L0_attn_setup():
        import jax, jax.numpy as jnp
        import numpy as np
        B, T, C = (2, 512, 256)
        NH = 16
        HS = C // NH
        BD = max(HS // 4, 16)
        HORIZON = 64
        key = jax.random.key(seed)
        ks = jax.random.split(key, 10)
        s = 0.02
        return {'x': jax.random.normal(ks[0], (B, T, C), dtype=jnp.float32), 'W_disp': jax.random.normal(ks[1], (NH * BD, C), dtype=jnp.float32) * s, 'W_val': jax.random.normal(ks[2], (C, C), dtype=jnp.float32) * s, 'rel_pos_emb': jax.random.normal(ks[3], (HORIZON, BD), dtype=jnp.float32) * s, 'strain_fused_w': jax.random.normal(ks[4], (2 * BD, BD), dtype=jnp.float32) * s, 'strain_fused_b': jnp.zeros((2 * BD,), dtype=jnp.float32), 'pos_proj_w': jax.random.normal(ks[5], (BD, BD), dtype=jnp.float32) * s, 'bond_out_w': jax.random.normal(ks[6], (1, BD), dtype=jnp.float32) * s, 'damage_out_w': jax.random.normal(ks[7], (1, BD), dtype=jnp.float32) * s, 'damage_out_b': jnp.full((1,), -3.0, dtype=jnp.float32), 'c_proj_w': jax.random.normal(ks[8], (C, C), dtype=jnp.float32) * s}
    _L0_attn_in = _L0_attn_setup()

    def _L0_ffn_setup():
        import jax, jax.numpy as jnp
        import numpy as np
        EMB = 256
        FF = 4 * EMB

        def _ternary(w):
            scale = jnp.maximum(jnp.mean(jnp.abs(w)), 1e-08)
            w_t = jnp.clip(jnp.round(w / scale), -1.0, 1.0)
            return w + jax.lax.stop_gradient(w_t - w)
        key = jax.random.key(seed)
        kx, k1, k2, kb1, kb2 = jax.random.split(key, 5)
        x = jax.random.normal(kx, (4, 512, EMB), dtype=jnp.float32)
        lim1 = 1.0 / np.sqrt(EMB)
        lim2 = 1.0 / np.sqrt(FF)
        W1 = jax.random.uniform(k1, (FF, EMB), jnp.float32, -lim1, lim1)
        b1 = jax.random.uniform(kb1, (FF,), jnp.float32, -lim1, lim1)
        W2 = jax.random.uniform(k2, (EMB, FF), jnp.float32, -lim2, lim2)
        b2 = jax.random.uniform(kb2, (EMB,), jnp.float32, -lim2, lim2)
        return {'x': x, 'W1': W1, 'b1': b1, 'W2': W2, 'b2': b2}
    _L0_ffn_in = _L0_ffn_setup()
    _d = {'L0_attn_x': _L0_attn_in['x'], 'L0_attn_W_disp': _L0_attn_in['W_disp'], 'L0_attn_W_val': _L0_attn_in['W_val'], 'L0_attn_rel_pos_emb': _L0_attn_in['rel_pos_emb'], 'L0_attn_strain_fused_w': _L0_attn_in['strain_fused_w'], 'L0_attn_strain_fused_b': _L0_attn_in['strain_fused_b'], 'L0_attn_pos_proj_w': _L0_attn_in['pos_proj_w'], 'L0_attn_bond_out_w': _L0_attn_in['bond_out_w'], 'L0_attn_damage_out_w': _L0_attn_in['damage_out_w'], 'L0_attn_damage_out_b': _L0_attn_in['damage_out_b'], 'L0_attn_c_proj_w': _L0_attn_in['c_proj_w'], 'L0_ffn_W1': _L0_ffn_in['W1'], 'L0_ffn_b1': _L0_ffn_in['b1'], 'L0_ffn_W2': _L0_ffn_in['W2'], 'L0_ffn_b2': _L0_ffn_in['b2']}
    _x0 = _d['L0_attn_x']
    _d['L0_attn_x'] = jax.random.normal(jax.random.fold_in(jax.random.key(seed), 1), (8, 512, 256), dtype=_x0.dtype)
    del _x0
    return _d

def reference(L0_attn_x, L0_attn_W_disp, L0_attn_W_val, L0_attn_rel_pos_emb, L0_attn_strain_fused_w, L0_attn_strain_fused_b, L0_attn_pos_proj_w, L0_attn_bond_out_w, L0_attn_damage_out_w, L0_attn_damage_out_b, L0_attn_c_proj_w, L0_ffn_W1, L0_ffn_b1, L0_ffn_W2, L0_ffn_b2):

    def _L0_attn_ref(x, W_disp, W_val, rel_pos_emb, strain_fused_w, strain_fused_b, pos_proj_w, bond_out_w, damage_out_w, damage_out_b, c_proj_w):
        import jax, jax.numpy as jnp
        import numpy as np
        B, T, C = (2, 512, 256)
        NH = 16
        HS = C // NH
        BD = max(HS // 4, 16)
        HORIZON = 64
        Bx, Tx, Cx = x.shape
        delta = min(HORIZON, Tx)
        gelu = lambda t: jax.nn.gelu(t, approximate=False)
        disp = (x @ W_disp.T).reshape(Bx, Tx, NH, BD).transpose(0, 2, 1, 3)
        val = (x @ W_val.T).reshape(Bx, Tx, NH, HS).transpose(0, 2, 1, 3)
        pad = ((0, 0), (0, 0), (delta - 1, 0), (0, 0))
        idx = jnp.arange(Tx)[:, None] + jnp.arange(delta)[None, :]
        disp_win = jnp.pad(disp, pad)[:, :, idx, :]
        strain = disp_win - disp[:, :, :, None, :]
        fused = strain @ strain_fused_w.T + strain_fused_b
        bond_feats, damage_feats = (fused[..., :BD], fused[..., BD:])
        pos_feat = rel_pos_emb[:delta] @ pos_proj_w.T
        bond_logits = (gelu(bond_feats + pos_feat) @ bond_out_w.T)[..., 0]
        damage = jax.nn.sigmoid((gelu(damage_feats) @ damage_out_w.T)[..., 0] + damage_out_b)
        logits = bond_logits - damage * 10.0
        cmask = jnp.arange(Tx)[:, None] - delta + 1 + jnp.arange(delta)[None, :] >= 0
        logits = jnp.where(cmask, logits, -jnp.inf)
        weights = jax.nn.softmax(logits, axis=-1)
        val_win = jnp.pad(val, pad)[:, :, idx, :]
        out = jnp.einsum('bhtw,bhtwd->bhtd', weights, val_win)
        out = out.transpose(0, 2, 1, 3).reshape(Bx, Tx, Cx)
        return out @ c_proj_w.T

    def _L0_ffn_ref(x, W1, b1, W2, b2):
        import jax, jax.numpy as jnp
        import numpy as np
        EMB = 256
        FF = 4 * EMB

        def _ternary(w):
            scale = jnp.maximum(jnp.mean(jnp.abs(w)), 1e-08)
            w_t = jnp.clip(jnp.round(w / scale), -1.0, 1.0)
            return w + jax.lax.stop_gradient(w_t - w)
        h = jnp.einsum('bsd,fd->bsf', x, _ternary(W1)) + b1
        h = jax.nn.gelu(h, approximate=False)
        out = jnp.einsum('bsf,df->bsd', h, _ternary(W2)) + b2
        return out
    x = L0_attn_x
    x = _layernorm(x + _L0_attn_ref(x, L0_attn_W_disp, L0_attn_W_val, L0_attn_rel_pos_emb, L0_attn_strain_fused_w, L0_attn_strain_fused_b, L0_attn_pos_proj_w, L0_attn_bond_out_w, L0_attn_damage_out_w, L0_attn_damage_out_b, L0_attn_c_proj_w), axis=-1)
    x = _layernorm(x + _L0_ffn_ref(x, L0_ffn_W1, L0_ffn_b1, L0_ffn_W2, L0_ffn_b2), axis=-1)
    return x

_drawn_inputs = setup_inputs


def setup_inputs(seed=0):
    import zlib

    import numpy as np

    out = dict(_drawn_inputs(seed))
    spreads = {'L0_attn_strain_fused_b': (0.0, 0.8)}
    factors = {'L0_attn_W_disp': 8.0,
     'L0_attn_W_val': 3.708,
     'L0_attn_rel_pos_emb': 30.63,
     'L0_attn_strain_fused_w': 8.0,
     'L0_attn_pos_proj_w': 38.443,
     'L0_attn_bond_out_w': 8.0,
     'L0_attn_damage_out_w': 8.0,
     'L0_attn_c_proj_w': 3.756,
     'L0_ffn_b1': 23.301,
     'L0_ffn_b2': 64.0}
    for name, (base, spread) in spreads.items():
        noise = np.random.default_rng([zlib.crc32(name.encode()), seed]).standard_normal(out[name].shape)
        drawn = base * np.exp(spread * noise) if base else spread * noise
        out[name] = jnp.asarray(drawn.astype(out[name].dtype))
    for name, factor in factors.items():
        out[name] = (out[name] * factor).astype(out[name].dtype)
    return out
```

```python
import concourse.bass as bass
from concourse import mybir
from concourse.alu_op_type import AluOpType as ALU
from contextlib import ExitStack

ACT = mybir.ActivationFunctionType
AX_X = mybir.AxisListType.X
F32 = mybir.dt.float32

P = 128
B, T, C = 8, 512, 256
NH, HS, BD = 16, 16, 16
W = 64
FF = 4 * C
EPS = 1e-5
HPG = P // (2 * BD)
HG = NH // HPG
CC = C // P
TB = T // P
KB = T // W
MS = W // 4
SLOTS = 8
BAND = 2 * W
VW = HS + 1
FC = FF // P
HALF = 2 * P
MAGIC = 1.5 * 2.0 ** 23
MASKED = -1e30

POOL_SLOTS = frozenset(w for w in range(W) if w % 8 in (2, 4, 7))


def on_vector(w):
    return sum(1 for v in range(w) if v not in POOL_SLOTS)


def on_pool(w):
    return w - on_vector(w)


ND, NP_ = on_vector(W), on_pool(W)


def gelu_groups():
    groups, w = [], 0
    while w < W:
        pair = w not in POOL_SLOTS and w % 4 < 3 and w + 1 not in POOL_SLOTS
        groups.append((w, 2 if pair else 1))
        w += groups[-1][1]
    return groups


GELUS = gelu_groups()
NG = len(GELUS)


def gelus_through(w):
    return sum(1 for first, _ in GELUS if first <= w)


def first_token(w):
    return W - 4 - 4 * (w // 4)


def post_ln_block(nc, xT, x_rows, w_disp, w_valT, relT, strain_wT, strain_b, pos_wT, bond_w, damage_w,
                  damage_b, c_projT, w1T, b1, w2T, b2, out):
    scratch = nc.dram_tensor("band_scratch", (KB, W, NH * BAND), F32, kind="Internal").ap()

    with ExitStack() as ctx:
        def sb(name, *shape):
            return ctx.enter_context(nc.sbuf_tensor(name, list(shape), F32))

        def sem(name):
            return ctx.enter_context(nc.semaphore(name))

        ring = sb("ring", P, SLOTS, HG, T)
        G = sb("G", P, HG, W + T)
        xg = sb("xg", P, CC, T)
        xv = sb("xv", P, CC, W + T)
        lg_sb = sb("lg_sb", P, 2, T)
        L = sb("L", P, TB * HG, 2, W, HPG)
        E_ = sb("E_", P, TB, NH, W)
        band = sb("band", P, 4, HPG, BAND)
        pt_sb = sb("pt_sb", P, 2, HPG, P)
        V1 = sb("V1", P, KB, NH, VW)
        o_sb = sb("o_sb", P, 2, C)
        oT_sb = sb("oT_sb", P, 2, CC, P)
        xt = sb("xt", P, TB, C)
        x1T = sb("x1T", P, CC, HALF)
        hT = sb("hT", P, FC, HALF)
        mx = sb("mx", P, TB * NH)
        rden = sb("rden", P, 2, NH)
        stats = sb("stats", P, 2 * TB, 6)
        mv = sb("mv", P, 2 * TB, 2)
        ve = sb("ve", P, 2 * TB)
        rstd = sb("rstd", P, 2 * TB)
        minus_half = sb("minus_half", P, 1)
        Wc = sb("Wc", P, CC, HG, P)
        wv = sb("wv", P, CC, C)
        cp = sb("cp", P, CC, C)
        w1 = sb("w1", P, CC, FF)
        w2 = sb("w2", P, FC, C)
        wlog = sb("wlog", P, 4, 32)
        ident = sb("ident", P, P)
        ones = sb("ones", P, P)
        mask = sb("mask", P, W)
        posb = sb("posb", P, W)
        sbias = sb("sbias", P, 1)
        dbias = sb("dbias", P, 2)
        b1_sb = sb("b1_sb", P, FC)
        b2_sb = sb("b2_sb", P, C)
        tern = sb("tern", P, 8)
        wd = ring[0:64, 0, 0:2, :].rearrange("p a b -> p (a b)").rearrange("p (g c) -> p g c", g=HG)
        bdiag = ring[0:64, 1, 0, 0:P]
        ppw = ring[0:16, 1, 1, 0:P].rearrange("p (h f) -> p h f", h=HPG)
        rel = ring[0:16, 1, 2, 0:W]
        wtmp = hT[:].rearrange("p a b -> p (a b)")

        def ps(name):
            return ctx.enter_context(nc.psum_tensor(name, [P, 512], F32))

        lg_ps = [ps("lg_ps0"), ps("lg_ps1")]
        lt_ps = ps("lt_ps")
        pt_ps = [ps("pt_ps0"), ps("pt_ps1")]
        o_ps = ps("o_ps")
        ms_ps = [ps("ms_ps0"), ps("ms_ps1")]
        g_ps = [pt_ps[0], pt_ps[1], o_ps, pt_ps[0]]

        loads_a, loads_b, loads_c = sem("loads_a"), sem("loads_b"), sem("loads_c")
        zeros_done, prep_done = sem("zeros_done"), sem("prep_done")
        wc_made, pos_made, tern_sum, tern_tot = sem("wc_made"), sem("pos_made"), sem("tern_sum"), sem("tern_tot")
        tern_step, tern_done = sem("tern_step"), sem("tern_done")
        scratch_zero = sem("scratch_zero")
        xg_in, xv_in, xt_in = sem("xg_in"), sem("xv_in"), sem("xt_in")
        g_full, g_evac = sem("g_full"), sem("g_evac")
        diff_dve, diff_pool = sem("diff_dve"), sem("diff_pool")
        gelu_done, slot_used = sem("gelu_done"), sem("slot_used")
        lg_evac = sem("lg_evac")
        lt_full, lt_evac = sem("lt_full"), sem("lt_evac")
        tanh_done, logit_done, masked = sem("tanh_done"), sem("logit_done"), sem("masked")
        max_done, sub_done, exp_done = sem("max_done"), sem("sub_done"), sem("exp_done")
        skew_out = sem("skew_out")
        band_in = [sem(f"band_in{i}") for i in range(4)]
        pt_full, pt_evac, pv_done = sem("pt_full"), sem("pt_evac"), sem("pv_done")
        den_done, o_norm = sem("den_done"), sem("o_norm")
        v_full, v_evac = sem("v_full"), sem("v_evac")
        ot_full, ot_evac = sem("ot_full"), sem("ot_evac")
        cp_full, sum_done, stat_done = sem("cp_full"), sem("sum_done"), sem("stat_done")
        aggr_done, ve_done, rstd_done = sem("aggr_done"), sem("ve_done"), sem("rstd_done")
        norm_done = sem("norm_done")
        xt_full, xt_evac, b2_added = sem("xt_full"), sem("xt_evac"), sem("b2_added")
        h_full, h_gelu = sem("h_full"), sem("h_gelu")
        f2_full = sem("f2_full")
        stored = sem("stored")

        def wait(eng, s, n):
            if not isinstance(n, int) or n > 0:
                eng.wait_ge(s, n)

        def batches(eng, body):
            body(0, main=True, post=False, ahead=True)
            body(1, main=True, post=True, ahead=True)
            with eng.Fori(2, B - 1) as j:
                body(j, main=True, post=True, ahead=True)
            body(B - 1, main=True, post=True, ahead=False)
            body(B, main=False, post=True, ahead=False)

        block = ctx.enter_context(nc.Block())

        @block.sync
        def _(sp):
            def load(dst, src, s):
                sp.dma_start(dst, src).then_inc(s, 16)

            load(wd, w_disp.rearrange("(g p) c -> p g c", p=64), loads_a)
            load(xg[:], xT[0].rearrange("(c p) t -> p c t", p=P), xg_in)
            load(rel, relT, loads_a)
            sp.wait_ge(zeros_done, 1)
            for h in range(HPG):
                load(bdiag[16 * h:16 * h + 16, 32 * h:32 * h + 32], strain_wT, loads_a)
                load(ppw[:, h, 0:16], pos_wT, loads_a)
                load(sbias[32 * h:32 * h + 32, :], strain_b.rearrange("(f a) -> f a", a=1), loads_a)
                for kind, src in ((0, bond_w), (1, damage_w)):
                    row = 32 * h + 16 * kind
                    dst = bass.AP(tensor=wlog[:].tensor, offset=row * 128 + 16 * kind + h, ap=[[128, 16], [36, 4], [1, 1]])
                    with nc.allow_non_contiguous_dma(reason="64 weights, once"):
                        load(dst, bass.AP(tensor=src.tensor, offset=0, ap=[[1, 16], [0, 4], [1, 1]]), loads_a)
            load(dbias[:, 0:1], damage_b.partition_broadcast(P), loads_b)
            load(b2_sb[:], b2.partition_broadcast(P), loads_b)
            load(b1_sb[:], b1, loads_b)
            load(wv[:], w_valT.rearrange("(c p) n -> p c n", p=P), loads_b)
            load(cp[:], c_projT.rearrange("(c p) n -> p c n", p=P), loads_b)
            load(w1[:], w1T.rearrange("(c p) n -> p c n", p=P), loads_c)
            load(w2[:], w2T.rearrange("(c p) n -> p c n", p=P), loads_c)
            sp.wait_ge(zeros_done, 2)
            ez = E_[:, :, :, :].rearrange("p a b c -> p (a b c)")
            zdst = scratch.rearrange("k r n -> (k r) n").rearrange("(a p) n -> p a n", p=P)
            for a in range(2):
                sp.dma_start(zdst[:, 2 * a:2 * a + 2, :], ez.rearrange("p (a n) -> p a n", a=2)).then_inc(scratch_zero, 16)

            def body(j, main, post, ahead):
                if ahead:
                    wait(sp, g_full, 4 * j + 4)
                    load(xg[:], xT[bass.ds(j + 1, 1)].rearrange("a (c p) t -> p (a c) t", p=P), xg_in)
                if not post:
                    sp.wait_ge(scratch_zero, 32)
                if post:
                    wait(sp, v_full, 4 * j - 4)
                    load(xv[:, :, W:W + T], xT[bass.ds(j - 1, 1)].rearrange("a (c p) t -> p (a c) t", p=P), xv_in)
                    wait(sp, stored, 16 * j - 16)
                    load(xt[:], x_rows[bass.ds(j - 1, 1)].rearrange("a (n p) c -> p (a n) c", p=P), xt_in)
                    wait(sp, exp_done, 1 * j)
                    wait(sp, pv_done, 16 * j - 16)
                    for tb in range(TB):
                        for half in range(2):
                            src = E_[64 * half:64 * half + 64, tb, :, :]
                            dst = bass.AP(tensor=scratch.tensor, offset=(2 * tb + half) * W * NH * BAND + 1,
                                          ap=[[NH * BAND + 1, W], [BAND, NH], [1, W]])
                            sp.dma_start(dst, src).then_inc(skew_out, 16)
                    wait(sp, skew_out, 128 * j)
                    for n in range(TB * HG):
                        tb, hg = n // HG, n % HG
                        wait(sp, pt_full, 16 * j - 16 + max(n - 3, 0))
                        src = scratch[2 * tb:2 * tb + 2, :, hg * HPG * BAND:(hg + 1) * HPG * BAND]
                        load(band[:, n % 4, :, :].rearrange("p h n -> p (h n)"),
                             src.rearrange("k r n -> (k r) n"), band_in[n % 4])
                    wait(sp, norm_done, 8 * j)
                    load(out[bass.ds(j - 1, 1)].rearrange("a (n p) c -> p (a n) c", p=P), xt[:], stored)

            batches(sp, body)
            sp.wait_ge(stored, 16 * B)

        @block.scalar
        def _(act):
            act.wait_ge(loads_b, 80)
            nc.scalar.mul(dbias[:, 1:2], dbias[:, 0:1], 0.5).then_inc(prep_done, 1)
            act.wait_ge(loads_c, 32)
            nc.scalar.activation(wtmp, w1[:].rearrange("p a b -> p (a b)"), ACT.Abs,
                                 accum_out=tern[:, 0:1]).then_inc(tern_sum, 1)
            act.wait_ge(tern_sum, 1)
            nc.scalar.activation(wtmp, w2[:].rearrange("p a b -> p (a b)"), ACT.Abs,
                                 accum_out=tern[:, 1:2]).then_inc(tern_sum, 1)

            def gelus(j, first, last):
                for w, n in GELUS:
                    if not first <= w < last:
                        continue
                    v = ring[:, w % SLOTS:w % SLOTS + n, :, first_token(w):T].rearrange("p s g t -> p (s g) t")
                    if w in POOL_SLOTS:
                        wait(act, diff_pool, NP_ * j + on_pool(w + n))
                        nc.scalar.activation(v, v, ACT.Gelu, bias=posb[:, w:w + 1]).then_inc(gelu_done, 1)
                    else:
                        wait(act, diff_dve, ND * j + on_vector(w + n))
                        nc.scalar.activation(v, v, ACT.Gelu).then_inc(gelu_done, 1)

            def hidden_gelu(j, n):
                wait(act, h_full, 8 * j - 8 + n + 1)
                if n >= 4:
                    wait(act, f2_full, 4 * j - 4 + 2)
                elif n == 0:
                    wait(act, f2_full, 4 * j - 4)
                for i in range(2):
                    f = 2 * (n % 4) + i
                    ins = nc.scalar.activation(hT[:, f, :], ms_ps[(n + 1 + n // 4) % 2][:, i * HALF:(i + 1) * HALF],
                                               ACT.Gelu, bias=b1_sb[:, f:f + 1])
                ins.then_inc(h_gelu, 1)

            def body(j, main, post, ahead):
                for m in range(MS):
                    if post and m == 2:
                        wait(act, lt_evac, 16 * j)
                        nc.scalar.activation(L[:, :, 1, :, :], L[:, :, 1, :, :], ACT.Tanh,
                                             bias=dbias[:, 1:2], scale=0.5).then_inc(tanh_done, 1)
                    if post and m == 4:
                        wait(act, sub_done, 1 * j)
                        e = E_[:].rearrange("p a b c -> p (a b c)")
                        nc.scalar.activation(e, e, ACT.Exp).then_inc(exp_done, 1)
                    if main:
                        gelus(j, 4 * m, 4 * m + 2)
                    if post and m in (12, 14):
                        hidden_gelu(j, 2 * m - 24)
                        hidden_gelu(j, 2 * m - 23)
                    if main:
                        gelus(j, 4 * m + 2, 4 * m + 4)
                    if post and m in (12, 14):
                        hidden_gelu(j, 2 * m - 22)
                        hidden_gelu(j, 2 * m - 21)

            act.wait_ge(prep_done, 5)
            act.wait_ge(pos_made, 2)
            batches(act, body)

        def strain_operands(w):
            k, lo = W - 1 - w, first_token(w)
            return ring[:, w % SLOTS, :, lo:T], G[:, :, W + lo - k:W + T - k], G[:, :, W + lo:W + T]

        @block.gpsimd
        def _(pool):
            nc.gpsimd.memset(ones[:], 1.0).then_inc(tern_step, 1)
            pool.wait_ge(tern_step, 1)
            nc.gpsimd.affine_select(out=ident[:], in_=ones[:], pattern=[[-1, P]], compare_op=ALU.is_equal, fill=0.0,
                                    base=0, channel_multiplier=1).then_inc(prep_done, 1)
            nc.gpsimd.memset(mask[:], 0.0).then_inc(tern_step, 1)
            pool.wait_ge(tern_step, 2)
            nc.gpsimd.affine_select(out=mask[:], in_=mask[:], pattern=[[1, W]], compare_op=ALU.is_ge, fill=MASKED,
                                    base=1 - W, channel_multiplier=1).then_inc(prep_done, 1)
            nc.gpsimd.memset(minus_half[:], -0.5).then_inc(prep_done, 1)
            nc.gpsimd.memset(V1[:, :, :, HS:VW], 1.0).then_inc(prep_done, 1)
            pool.wait_ge(prep_done, 5)

            def strains(j, m):
                for w in range(4 * m, 4 * m + 4):
                    if w in POOL_SLOTS:
                        wait(pool, g_evac, 4 * j + 4)
                        wait(pool, slot_used, 64 * j + w - SLOTS + 1)
                        out_w, past, now = strain_operands(w)
                        nc.gpsimd.tensor_tensor(out_w, past, now, ALU.subtract).then_inc(diff_pool, 1)

            def rstd_of(j, n):
                wait(pool, ve_done, 8 * j - 8 + n + 1)
                nc.gpsimd.tensor_tensor(rstd[:, n:n + 1], ve[:, n:n + 1], minus_half[:], ALU.pow).then_inc(rstd_done, 1)

            def add_b2(j, half):
                wait(pool, xt_full, 2 * j - 2 + half + 1)
                for n in range(2):
                    ins = nc.gpsimd.tensor_tensor(xt[:, 2 * half + n, :], xt[:, 2 * half + n, :], b2_sb[:], ALU.add)
                ins.then_inc(b2_added, 1)

            def body(j, main, post, ahead):
                for m in range(MS):
                    if post and m == 3:
                        wait(pool, logit_done, 1 * j)
                        nc.gpsimd.tensor_tensor(E_[:, 0, :, :], E_[:, 0, :, :],
                                                mask[:].unsqueeze(1).to_broadcast([P, NH, W]),
                                                ALU.add).then_inc(masked, 1)
                    if post and 9 <= m < 13:
                        rstd_of(j, m - 9)
                    if post and m == 12:
                        add_b2(j, 0)
                    if post and m == 14:
                        rstd_of(j, 4)
                        rstd_of(j, 5)
                        add_b2(j, 1)
                    if main and m < MS - 1:
                        strains(j, m + 1)
                    if ahead and m == MS - 1:
                        strains(j + 1, 0)
                    if post and m == MS - 1:
                        rstd_of(j, 6)
                        rstd_of(j, 7)

            pool.wait_ge(pos_made, 2)
            strains(0, 0)
            batches(pool, body)

        @block.vector
        def _(dve):
            for z in (ring[0:64, 1, 0, 0:P], ring[0:16, 1, 1, 0:P], wlog[:]):
                ins = nc.vector.memset(z, 0.0)
            ins.then_inc(zeros_done, 1)
            nc.vector.memset(E_[:], 0.0).then_inc(zeros_done, 1)
            for z in (G[:, :, 0:W], xv[:, :, 0:W], lg_ps[0][:], lg_ps[1][:]):
                ins = nc.vector.memset(z, 0.0)
            ins.then_inc(zeros_done, 1)

            dve.wait_ge(wc_made, 1)
            for c in range(CC):
                ins = nc.vector.tensor_copy(Wc[:, c, :, :].rearrange("p g n -> p (g n)"), ms_ps[c][:])
            ins.then_inc(wc_made, 1)
            dve.wait_ge(pos_made, 1)
            nc.vector.tensor_scalar(posb[:], lt_ps[:, 0:W], sbias[:, 0:1], None, ALU.add).then_inc(pos_made, 1)

            def ternary():
                def step(ins):
                    steps[0] += 1
                    ins.then_inc(tern_step, 1)
                    dve.wait_ge(tern_step, steps[0])

                steps = [2]
                dve.wait_ge(tern_tot, 1)
                step(nc.vector.tensor_scalar(tern[:, 2:4], o_ps[:, 0:2], 1.0 / (FF * C), 1e-8, ALU.mult, ALU.max))
                step(nc.vector.reciprocal(tern[:, 4:6], tern[:, 2:4]))
                for n, wt in enumerate((w1, w2)):
                    v = wt[:].rearrange("p a b -> p (a b)")
                    r = wtmp
                    step(nc.vector.tensor_scalar(r, v, tern[:, 4 + n:5 + n], MAGIC, ALU.mult, ALU.add))
                    step(nc.vector.tensor_scalar(r, r, MAGIC, 1.0, ALU.subtract, ALU.min))
                    step(nc.vector.scalar_tensor_tensor(out=r, in0=r, scalar=-1.0, in1=v, op0=ALU.max, op1=ALU.subtract))
                    step(nc.vector.tensor_tensor(v, v, r, ALU.add))
                nc.vector.tensor_copy(tern[:, 6:7], tern[:, 4:5]).then_inc(tern_done, 1)

            def g_copy(j):
                for hg in range(HG):
                    wait(dve, g_full, 4 * j + hg + 1)
                    if hg == 0:
                        wait(dve, diff_pool, NP_ * j)
                        wait(dve, diff_dve, ND * j)
                    nc.vector.tensor_copy(G[:, hg, W:W + T], g_ps[hg][:]).then_inc(g_evac, 1)
                wait(dve, g_evac, 4 * j + 4)

            def strain(j, w):
                wait(dve, slot_used, 64 * j + w - SLOTS + 1)
                out_w, past, now = strain_operands(w)
                nc.vector.scalar_tensor_tensor(out=out_w, in0=past, scalar=posb[:, w:w + 1], in1=now, op0=ALU.add,
                                               op1=ALU.subtract).then_inc(diff_dve, 1)

            def logits_out(j, m):
                wait(dve, slot_used, 64 * j + 4 * m + 4)
                wait(dve, lt_full, 16 * j + m - 1)
                nc.vector.tensor_copy(lg_sb[:, m % 2, :], lg_ps[m % 2][:]).then_inc(lg_evac, 1)

            def logits_turned(j, m):
                wait(dve, lt_full, 16 * j + m + 1)
                if m == 0:
                    wait(dve, logit_done, 1 * j)
                nc.vector.tensor_copy(L[:, :, :, 4 * m:4 * m + 4, :].rearrange("p g y w h -> p g y (w h)"),
                                      lt_ps[:].rearrange("p (g y r) -> p g y r", g=TB * HG, y=2)).then_inc(lt_evac, 1)

            e_rows = E_[:].rearrange("p a b c -> p (a b) c")

            def combine(j):
                wait(dve, tanh_done, 1 * j)
                wait(dve, skew_out, 128 * j - 128)
                for h in range(HPG):
                    ins = nc.vector.scalar_tensor_tensor(
                        out=E_[:].rearrange("p a (g h) w -> p (a g) h w", h=HPG)[:, :, h, :], in0=L[:, :, 1, :, h],
                        scalar=-5.0, in1=L[:, :, 0, :, h], op0=ALU.mult, op1=ALU.add)
                ins.then_inc(logit_done, 1)

            def less_maximum(j):
                wait(dve, masked, 1 * j)
                nc.vector.tensor_reduce(mx[:], e_rows, AX_X, ALU.max).then_inc(max_done, 1)
                wait(dve, max_done, 1 * j)
                nc.vector.tensor_tensor(e_rows, e_rows, mx[:].unsqueeze(2).to_broadcast([P, TB * NH, W]),
                                        ALU.subtract).then_inc(sub_done, 1)

            def values_out(j, n):
                wait(dve, v_full, 4 * j - 4 + n + 1)
                nc.vector.tensor_copy(V1[:, 2 * n:2 * n + 2, :, 0:HS].rearrange("p k h d -> p (k h) d"),
                                      ms_ps[n % 2][:].rearrange("p (k d) -> p k d", d=HS)).then_inc(v_evac, 1)

            def band_turned(j, n):
                wait(dve, pt_full, 16 * j - 16 + n + 1)
                wait(dve, pv_done, 16 * j - 16 + max(n - 1, 0))
                nc.vector.tensor_copy(pt_sb[:, n % 2, :, :].rearrange("p h t -> p (h t)"),
                                      pt_ps[n % 2][:]).then_inc(pt_evac, 1)

            def attention_out(j, tb):
                o = o_ps[:, 0:NH * VW].rearrange("p (h d) -> p h d", d=VW)
                wait(dve, pv_done, 16 * j - 16 + 4 * tb + 4)
                nc.vector.reciprocal(rden[:, tb % 2, :], o[:, :, HS]).then_inc(den_done, 1)
                wait(dve, den_done, 4 * j - 4 + tb + 1)
                wait(dve, ot_full, 4 * j - 4 + max(tb - 1, 0))
                nc.vector.tensor_tensor(o_sb[:, tb % 2, :].rearrange("p (h d) -> p h d", d=HS), o[:, :, 0:HS],
                                        rden[:, tb % 2, :].unsqueeze(2).to_broadcast([P, NH, HS]),
                                        ALU.mult).then_inc(o_norm, 1)

            def attention_turned(j, tb):
                wait(dve, ot_full, 4 * j - 4 + tb + 1)
                wait(dve, cp_full, 4 * j - 4 + max(tb - 1, 0))
                nc.vector.tensor_copy(oT_sb[:, tb % 2, :, :].rearrange("p c t -> p (c t)"),
                                      ms_ps[0][:, 0:CC * P]).then_inc(ot_evac, 1)

            def sum_and_stats(j, n, product, arrived, value):
                row = xt[:, n % TB, :]
                wait(dve, arrived, value)
                nc.vector.tensor_tensor(row, product, row, ALU.add).then_inc(sum_done, 1)
                wait(dve, sum_done, 8 * j - 8 + n + 1)
                nc.vector.bn_stats(stats[:, n, :], row).then_inc(stat_done, 1)
                dve.wait_ge(zeros_done, 3)
                wait(dve, stat_done, 8 * j - 8 + n + 1)
                nc.vector.bn_aggr(mv[:, n, :], stats[:, n, :]).then_inc(aggr_done, 1)
                wait(dve, aggr_done, 8 * j - 8 + n + 1)
                nc.vector.tensor_scalar(ve[:, n:n + 1], mv[:, n, 1:2], EPS, None, ALU.add).then_inc(ve_done, 1)

            def normalise(j, n):
                wait(dve, rstd_done, 8 * j - 8 + n + 1)
                nc.vector.tensor_scalar(xt[:, n % TB, :], xt[:, n % TB, :], mv[:, n, 0:1], rstd[:, n:n + 1],
                                        ALU.subtract, ALU.mult).then_inc(norm_done, 1)

            def tokens_turned(j, half):
                wait(dve, xt_full, 2 * j - 2 + half + 1)
                if half:
                    wait(dve, h_full, 8 * j - 8 + 4)
                nc.vector.tensor_copy(x1T[:].rearrange("p c (n t) -> p n c t", n=2),
                                      ms_ps[half][:].rearrange("p (n c t) -> p n c t", n=2, c=CC)).then_inc(xt_evac, 1)

            def body(j, main, post, ahead):
                for m in range(MS):
                    if post and m == 0:
                        logits_out(j - 1, MS - 1)
                        logits_turned(j - 1, MS - 2)
                    if post and m == 1:
                        logits_turned(j - 1, MS - 1)
                    if post and m == 2:
                        combine(j)
                    if main and m >= 1:
                        logits_out(j, m - 1)
                    if main and m >= 2:
                        logits_turned(j, m - 2)
                    if post and m == 3:
                        less_maximum(j)
                    if post and m in (4, 5):
                        values_out(j, 2 * (m - 4))
                        values_out(j, 2 * (m - 4) + 1)
                    if ahead and m == MS - 1:
                        g_copy(j + 1)
                    todo = [w for w in range(4 * m + 4, 4 * m + 8) if w % W not in POOL_SLOTS]
                    for i in range(4):
                        if post and 7 <= m < 11:
                            band_turned(j, 4 * (m - 7) + i)
                        if i < len(todo):
                            w = todo[i]
                            if main and m < MS - 1:
                                strain(j, w)
                            if ahead and m == MS - 1:
                                strain(j + 1, w - W)
                        if post and 8 <= m < 12 and i == 1:
                            attention_turned(j, m - 8)
                        if post and 8 <= m < 12 and i == 3:
                            wait(dve, xt_in, 16 * j)
                            sum_and_stats(j, m - 8, ms_ps[1][:, 0:C], cp_full, 4 * j - 4 + m - 8 + 1)
                        if post and 9 <= m < 13 and i == 0:
                            normalise(j, m - 9)
                    if post and 7 <= m < 11:
                        attention_out(j, m - 7)
                    if post and m == 11:
                        tokens_turned(j, 0)
                    if post and m == 13:
                        wait(dve, b2_added, 2 * j - 1)
                        sum_and_stats(j, 4, ms_ps[1][:, 0:C], f2_full, 4 * j - 4 + 1)
                        sum_and_stats(j, 5, ms_ps[0][:, 0:C], f2_full, 4 * j - 4 + 2)
                        tokens_turned(j, 1)
                    if post and m == 14:
                        normalise(j, 4)
                        normalise(j, 5)
                    if post and m == 15:
                        wait(dve, b2_added, 2 * j)
                        sum_and_stats(j, 6, ms_ps[0][:, 0:C], f2_full, 4 * j - 4 + 3)
                        sum_and_stats(j, 7, ms_ps[1][:, 0:C], f2_full, 4 * j - 4 + 4)
                        normalise(j, 6)
                        normalise(j, 7)
                    if not post and m == 6:
                        ternary()
                        dve.wait_ge(scratch_zero, 32)

            g_copy(0)
            for w in range(4):
                if w not in POOL_SLOTS:
                    strain(0, w)
            batches(dve, body)

        @block.tensor
        def _(pe):
            pe.wait_ge(loads_a, 16 * (2 + 5 * HPG))
            pe.wait_ge(zeros_done, 3)
            for c in range(CC):
                for hg in range(HG):
                    ins = nc.tensor.matmul(ms_ps[c][:, hg * P:(hg + 1) * P], wd[:, hg, c * P:(c + 1) * P], bdiag,
                                           start=True, stop=True)
            ins.then_inc(wc_made, 1)
            nc.tensor.matmul(lt_ps[:, 0:W], ppw.rearrange("p h f -> p (h f)"), rel, start=True,
                             stop=True).then_inc(pos_made, 1)
            pe.wait_ge(wc_made, 2)

            def project_g(j, hg):
                if hg == 0:
                    wait(pe, xg_in, 16 * j + 16)
                    wait(pe, pt_evac, 16 * j - 16)
                if hg == 2:
                    wait(pe, o_norm, 4 * j - 4)
                if hg == 3:
                    wait(pe, g_evac, 4 * j + 1)
                for c in range(CC):
                    ins = nc.tensor.matmul(g_ps[hg][:], Wc[:, c, hg, :], xg[:, c, :], start=(c == 0), stop=(c == CC - 1))
                ins.then_inc(g_full, 1)

            def slot_logits(j, w):
                wait(pe, gelu_done, NG * j + gelus_through(w))
                m, s = w // 4, w % 4
                if s == 0:
                    wait(pe, lg_evac, 16 * j + m - 1)
                lo = first_token(w)
                for hg in range(HG):
                    ins = nc.tensor.matmul(lg_ps[m % 2][32 * hg:32 * hg + 32, lo:T], wlog[:, s, :],
                                           ring[:, w % SLOTS, hg, lo:T], start=(s == 0), stop=(s == 3))
                ins.then_inc(slot_used, 1)

            def turn_logits(j, m):
                wait(pe, lg_evac, 16 * j + m + 1)
                wait(pe, lt_evac, 16 * j + m)
                for tb in range(TB):
                    ins = nc.tensor.transpose(lt_ps[:, tb * P:(tb + 1) * P], lg_sb[:, m % 2, tb * P:(tb + 1) * P], ident[:])
                ins.then_inc(lt_full, 1)

            def values(j, n):
                if n == 0:
                    wait(pe, xv_in, 16 * j)
                if n < 2:
                    wait(pe, sum_done, 8 * j - 8)
                else:
                    wait(pe, v_evac, 4 * j - 4 + n - 1)
                for i in range(2):
                    kb = 2 * n + i
                    for c in range(CC):
                        ins = nc.tensor.matmul(ms_ps[n % 2][:, i * C:(i + 1) * C], xv[:, c, W * kb:W * kb + P],
                                               wv[:, c, :], start=(c == 0), stop=(c == CC - 1))
                ins.then_inc(v_full, 1)

            def turn_band(j, n, main):
                wait(pe, band_in[n % 4], 64 * j - 64 + 16 * (n // 4) + 16)
                if n < 2:
                    wait(pe, g_evac, 4 * j + 4 * main)
                else:
                    wait(pe, pt_evac, 16 * j - 16 + n - 1)
                for h in range(HPG):
                    ins = nc.tensor.transpose(pt_ps[n % 2][:, h * P:(h + 1) * P], band[:, n % 4, h, :], ident[:])
                ins.then_inc(pt_full, 1)

            def weigh_values(j, n):
                tb, hg = n // HG, n % HG
                wait(pe, pt_evac, 16 * j - 16 + n + 1)
                if n == 0:
                    wait(pe, v_evac, 4 * j)
                if hg == 0:
                    wait(pe, o_norm, 4 * j - 4 + tb)
                for h in range(HPG):
                    for half in range(2):
                        col = (hg * HPG + h) * VW
                        ins = nc.tensor.matmul(o_ps[64 * half:64 * half + 64, col:col + VW],
                                               pt_sb[:, n % 2, h, 64 * half:64 * half + 64],
                                               V1[:, 2 * tb + half, hg * HPG + h, :], start=True, stop=True)
                ins.then_inc(pv_done, 1)

            def turn_attention(j, tb):
                wait(pe, o_norm, 4 * j - 4 + tb + 1)
                if tb == 0:
                    wait(pe, v_evac, 4 * j)
                for c in range(CC):
                    ins = nc.tensor.transpose(ms_ps[0][:, c * P:(c + 1) * P], o_sb[:, tb % 2, c * P:(c + 1) * P], ident[:])
                ins.then_inc(ot_full, 1)

            def project_attention(j, tb):
                wait(pe, ot_evac, 4 * j - 4 + tb + 1)
                wait(pe, sum_done, 8 * j - 8 + tb)
                for c in range(CC):
                    ins = nc.tensor.matmul(ms_ps[1][:, 0:C], oT_sb[:, tb % 2, c, :], cp[:, c, :],
                                           start=(c == 0), stop=(c == CC - 1))
                ins.then_inc(cp_full, 1)

            def turn_tokens(j, half):
                wait(pe, norm_done, 8 * j - 8 + 2 * half + 2)
                if half == 0:
                    wait(pe, ot_evac, 4 * j)
                else:
                    wait(pe, sum_done, 8 * j - 8 + 5)
                for n in range(2):
                    for c in range(CC):
                        ins = nc.tensor.transpose(ms_ps[half][:, (n * CC + c) * P:(n * CC + c + 1) * P],
                                                  xt[:, 2 * half + n, c * P:(c + 1) * P], ident[:])
                ins.then_inc(xt_full, 1)

            def hidden(j, n):
                if n in (0, 4):
                    wait(pe, xt_evac, 2 * j - 2 + n // 4 + 1)
                    wait(pe, sum_done, 8 * j - 8 + (4 if n == 0 else 6))
                if n % 4 >= 2:
                    wait(pe, h_gelu, 8 * j - 8 + n - 1)
                for i in range(2):
                    f = 2 * (n % 4) + i
                    for c in range(CC):
                        ins = nc.tensor.matmul(ms_ps[(n + 1 + n // 4) % 2][:, i * HALF:(i + 1) * HALF],
                                               w1[:, c, f * P:(f + 1) * P], x1T[:, c, :],
                                               start=(c == 0), stop=(c == CC - 1))
                ins.then_inc(h_full, 1)

            def feed_out(j, n):
                wait(pe, h_gelu, 8 * j - 8 + 4 * (n // 2) + 4)
                bank = (1, 0, 0, 1)[n]
                for f in range(FC):
                    ins = nc.tensor.matmul(ms_ps[bank][:, 0:C], hT[:, f, (n % 2) * P:(n % 2 + 1) * P], w2[:, f, :],
                                           start=(f == 0), stop=(f == FC - 1))
                ins.then_inc(f2_full, 1)

            def body(j, main, post, ahead):
                for m in range(MS):
                    for s in range(4):
                        if post and 7 <= m < 11:
                            turn_band(j, 4 * (m - 7) + s, main)
                        if main:
                            slot_logits(j, 4 * m + s)
                        if s == 1 and post and m == 0:
                            turn_logits(j - 1, MS - 1)
                        if s == 1 and main and m >= 1:
                            turn_logits(j, m - 1)
                        if post and m in (4, 5) and s in (1, 3):
                            values(j, 2 * (m - 4) + s // 2)
                        if post and 7 <= m < 11:
                            weigh_values(j, 4 * (m - 7) + s)
                        if post and 8 <= m < 12 and s == 0:
                            turn_attention(j, m - 8)
                        if post and 8 <= m < 12 and s == 1:
                            project_attention(j, m - 8)
                        if post and m == 11 and s == 3:
                            turn_tokens(j, 0)
                        if post and m == 12 and s in (0, 2):
                            hidden(j, s)
                            hidden(j, s + 1)
                        if post and m == 13 and s in (0, 1):
                            feed_out(j, s)
                        if post and m == 13 and s == 2:
                            turn_tokens(j, 1)
                        if post and m == 13 and s == 3:
                            hidden(j, 4)
                            hidden(j, 5)
                        if post and m == 14 and s == 1:
                            hidden(j, 6)
                            hidden(j, 7)
                        if post and m == 14 and s == 3:
                            feed_out(j, 2)
                        if post and m == 15 and s == 1:
                            feed_out(j, 3)
                        if ahead and m == 14 and s < 3:
                            project_g(j + 1, s)
                        if ahead and m == 15 and s == 0:
                            project_g(j + 1, 3)
                    if not post and m == 13:
                        pe.wait_ge(tern_done, 1)
                    if not post and m == 3:
                        pe.wait_ge(g_evac, HG)
                        pe.wait_ge(tern_sum, 2)
                        nc.tensor.matmul(o_ps[:, 0:2], ones[:], tern[:, 0:2], start=True, stop=True).then_inc(tern_tot, 1)

            for hg in range(HG):
                project_g(0, hg)
            pe.wait_ge(prep_done, 5)
            pe.wait_ge(loads_b, 80)
            batches(pe, body)


def kernel(**inputs):
    import numpy as np
    import concourse.bacc as bacc
    from concourse.bass_utils import run_bass_kernel_spmd

    x = np.asarray(inputs["L0_attn_x"])
    def t(name):
        return np.ascontiguousarray(np.asarray(inputs[name]).T)

    data = {
        "xT": np.ascontiguousarray(x.transpose(0, 2, 1)),
        "x_rows": np.ascontiguousarray(x),
        "w_disp": np.ascontiguousarray(inputs["L0_attn_W_disp"]),
        "w_valT": t("L0_attn_W_val"),
        "relT": t("L0_attn_rel_pos_emb"),
        "strain_wT": t("L0_attn_strain_fused_w"),
        "strain_b": np.ascontiguousarray(inputs["L0_attn_strain_fused_b"]),
        "pos_wT": t("L0_attn_pos_proj_w"),
        "bond_w": np.ascontiguousarray(inputs["L0_attn_bond_out_w"]),
        "damage_w": np.ascontiguousarray(inputs["L0_attn_damage_out_w"]),
        "damage_b": np.ascontiguousarray(inputs["L0_attn_damage_out_b"]),
        "c_projT": t("L0_attn_c_proj_w"),
        "w1T": t("L0_ffn_W1"),
        "b1": np.ascontiguousarray(np.asarray(inputs["L0_ffn_b1"]).reshape(FC, P).T),
        "w2T": t("L0_ffn_W2"),
        "b2": np.ascontiguousarray(inputs["L0_ffn_b2"]),
    }
    nc = bacc.Bacc("TRN2", target_bir_lowering=False, num_devices=1)
    arrays = {f"in_{n}": a for n, a in data.items()}
    args = [nc.dram_tensor(f"in_{n}", a.shape, mybir.dt.from_np(a.dtype), kind="ExternalInput").ap()
            for n, a in data.items()]
    result = nc.dram_tensor("out_0", (B, T, C), F32, kind="ExternalOutput").ap()
    post_ln_block(nc, *args, result)
    r = run_bass_kernel_spmd(nc, [arrays], core_ids=[0])
    return r.results[0]["out_0"]
```

```python
import concourse.bass as bass
from concourse import mybir
from concourse.alu_op_type import AluOpType as ALU
from contextlib import ExitStack

ACT = mybir.ActivationFunctionType
AX_X = mybir.AxisListType.X
F32 = mybir.dt.float32

P = 128
B, T, C = 8, 512, 256
NH, HS, BD = 16, 16, 16
W = 64
FF = 4 * C
EPS = 1e-5
HPG = P // (2 * BD)
HG = NH // HPG
CC = C // P
TB = T // P
KB = T // W
MS = W // 4
SLOTS = 8
BAND = 2 * W
VW = HS + 1
FC = FF // P
HALF = 2 * P
LEAD = 6
TANH, COMBINE, MASK, MAXIMUM, EXP = 5, 7, 9, 10, 15
VALUES = 9
BANDS = 21
TURN0, HIDDEN0, FEED0, TURN1, NEXT_G, HIDDEN1, FEED1 = 46, 48, 54, 57, 54, 60, 65
MAGIC = 1.5 * 2.0 ** 23
MASKED = -1e30

POOL_SLOTS = frozenset(w for w in range(W) if w % 8 in (2, 4, 7))


def on_vector(w):
    return sum(1 for v in range(w) if v not in POOL_SLOTS)


def on_pool(w):
    return w - on_vector(w)


ND, NP_ = on_vector(W), on_pool(W)


def gelu_groups():
    groups, w = [], 0
    while w < W:
        pair = w not in POOL_SLOTS and w % 4 < 3 and w + 1 not in POOL_SLOTS
        groups.append((w, 2 if pair else 1))
        w += groups[-1][1]
    return groups


GELUS = gelu_groups()
NG = len(GELUS)


def gelus_through(w):
    return sum(1 for first, _ in GELUS if first <= w)


def first_token(w):
    return W - 4 - 4 * (w // 4)


def post_ln_block(nc, xT, x_rows, w_disp, w_valT, relT, strain_wT, strain_b, pos_wT, bond_w, damage_w,
                  damage_b, c_projT, w1T, b1, w2T, b2, out):
    scratch = nc.dram_tensor("band_scratch", (KB, W, NH * BAND), F32, kind="Internal").ap()

    with ExitStack() as ctx:
        def sb(name, *shape):
            return ctx.enter_context(nc.sbuf_tensor(name, list(shape), F32))

        def sem(name):
            return ctx.enter_context(nc.semaphore(name))

        ring = sb("ring", P, SLOTS, HG, T)
        G = sb("G", P, HG, W + T)
        xg = sb("xg", P, CC, T)
        xv = sb("xv", P, CC, W + T)
        lg_sb = sb("lg_sb", P, 2, T)
        L = sb("L", P, TB * HG, 2, W, HPG)
        E_ = sb("E_", P, TB, NH, W)
        band = sb("band", P, 4, HPG, BAND)
        pt_sb = sb("pt_sb", P, 2, HPG, P)
        V1 = sb("V1", P, KB, NH, VW)
        o_sb = sb("o_sb", P, 2, C)
        oT_sb = sb("oT_sb", P, 2, CC, P)
        xt = sb("xt", P, TB, C)
        x1T = sb("x1T", P, CC, HALF)
        hT = sb("hT", P, FC, HALF)
        mx = sb("mx", P, TB * NH)
        rden = sb("rden", P, 2, NH)
        stats = sb("stats", P, 2 * TB, 6)
        mv = sb("mv", P, 2 * TB, 2)
        ve = sb("ve", P, 2 * TB)
        rstd = sb("rstd", P, 2 * TB)
        minus_half = sb("minus_half", P, 1)
        Wc = sb("Wc", P, CC, HG, P)
        wv = sb("wv", P, CC, C)
        cp = sb("cp", P, CC, C)
        w1 = sb("w1", P, CC, FF)
        w2 = sb("w2", P, FC, C)
        wlog = sb("wlog", P, 4, 32)
        ident = sb("ident", P, P)
        ones = sb("ones", P, P)
        mask = sb("mask", P, W)
        posb = sb("posb", P, W)
        sbias = sb("sbias", P, 1)
        dbias = sb("dbias", P, 2)
        b1_sb = sb("b1_sb", P, FC)
        b2_sb = sb("b2_sb", P, C)
        tern = sb("tern", P, 8)
        wd = ring[0:64, 0, 0:2, :].rearrange("p a b -> p (a b)").rearrange("p (g c) -> p g c", g=HG)
        bdiag = ring[0:64, 1, 0, 0:P]
        ppw = ring[0:16, 1, 1, 0:P].rearrange("p (h f) -> p h f", h=HPG)
        rel = ring[0:16, 1, 2, 0:W]
        wtmp = hT[:].rearrange("p a b -> p (a b)")

        def ps(name):
            return ctx.enter_context(nc.psum_tensor(name, [P, 512], F32))

        lg_ps = [ps("lg_ps0"), ps("lg_ps1")]
        lt_ps = ps("lt_ps")
        pt_ps = [ps("pt_ps0"), ps("pt_ps1")]
        o_ps = ps("o_ps")
        ms_ps = [ps("ms_ps0"), ps("ms_ps1")]
        g_ps = [pt_ps[0], pt_ps[1], o_ps, ms_ps[1]]

        loads_a, loads_b, loads_c = sem("loads_a"), sem("loads_b"), sem("loads_c")
        zeros_done, prep_done = sem("zeros_done"), sem("prep_done")
        wc_made, pos_made, tern_sum, tern_tot = sem("wc_made"), sem("pos_made"), sem("tern_sum"), sem("tern_tot")
        tern_step, tern_done = sem("tern_step"), sem("tern_done")
        scratch_zero = sem("scratch_zero")
        xg_in, xv_in, xt_in = sem("xg_in"), sem("xv_in"), sem("xt_in")
        g_full, g_evac = sem("g_full"), sem("g_evac")
        diff_dve, diff_pool = sem("diff_dve"), sem("diff_pool")
        gelu_done, slot_used = sem("gelu_done"), sem("slot_used")
        lg_evac = sem("lg_evac")
        lt_full, lt_evac = sem("lt_full"), sem("lt_evac")
        tanh_done, logit_done, masked = sem("tanh_done"), sem("logit_done"), sem("masked")
        max_done, sub_done, exp_done = sem("max_done"), sem("sub_done"), sem("exp_done")
        skew_out = [sem(f"skew_out{i}") for i in range(TB)]
        band_in = [sem(f"band_in{i}") for i in range(4)]
        pt_full, pt_evac, pv_done = sem("pt_full"), sem("pt_evac"), sem("pv_done")
        den_done, o_norm = sem("den_done"), sem("o_norm")
        v_full, v_evac = sem("v_full"), sem("v_evac")
        ot_full, ot_evac = sem("ot_full"), sem("ot_evac")
        cp_full, sum_done, stat_done = sem("cp_full"), sem("sum_done"), sem("stat_done")
        aggr_done, ve_done, rstd_done = sem("aggr_done"), sem("ve_done"), sem("rstd_done")
        norm_done = sem("norm_done")
        xt_full, xt_evac, b2_added = sem("xt_full"), sem("xt_evac"), sem("b2_added")
        h_full, h_gelu = sem("h_full"), sem("h_gelu")
        f2_full = sem("f2_full")
        stored = sem("stored")

        def wait(eng, s, n):
            if not isinstance(n, int) or n > 0:
                eng.wait_ge(s, n)

        def batches(eng, body):
            body(0, main=True, post=False, late=False, ahead=True)
            body(1, main=True, post=True, late=False, ahead=True)
            with eng.Fori(2, B - 1) as j:
                body(j, main=True, post=True, late=True, ahead=True)
            body(B - 1, main=True, post=True, late=True, ahead=False)
            body(B, main=False, post=True, late=True, ahead=False)
            body(B + 1, main=False, post=False, late=True, ahead=False)

        def due(j, step, at, post, late):
            if post and step == at:
                return j - 1
            if late and step == at - W:
                return j - 2
            return None

        block = ctx.enter_context(nc.Block())

        @block.sync
        def _(sp):
            def load(dst, src, s):
                sp.dma_start(dst, src).then_inc(s, 16)

            load(wd, w_disp.rearrange("(g p) c -> p g c", p=64), loads_a)
            load(xg[:], xT[0].rearrange("(c p) t -> p c t", p=P), xg_in)
            load(rel, relT, loads_a)
            sp.wait_ge(zeros_done, 1)
            for h in range(HPG):
                load(bdiag[16 * h:16 * h + 16, 32 * h:32 * h + 32], strain_wT, loads_a)
                load(ppw[:, h, 0:16], pos_wT, loads_a)
                load(sbias[32 * h:32 * h + 32, :], strain_b.rearrange("(f a) -> f a", a=1), loads_a)
                for kind, src in ((0, bond_w), (1, damage_w)):
                    row = 32 * h + 16 * kind
                    dst = bass.AP(tensor=wlog[:].tensor, offset=row * 128 + 16 * kind + h, ap=[[128, 16], [36, 4], [1, 1]])
                    with nc.allow_non_contiguous_dma(reason="64 weights, once"):
                        load(dst, bass.AP(tensor=src.tensor, offset=0, ap=[[1, 16], [0, 4], [1, 1]]), loads_a)
            load(dbias[:, 0:1], damage_b.partition_broadcast(P), loads_b)
            load(b2_sb[:], b2.partition_broadcast(P), loads_b)
            load(b1_sb[:], b1, loads_b)
            load(wv[:], w_valT.rearrange("(c p) n -> p c n", p=P), loads_b)
            load(cp[:], c_projT.rearrange("(c p) n -> p c n", p=P), loads_b)
            load(w1[:], w1T.rearrange("(c p) n -> p c n", p=P), loads_c)
            load(w2[:], w2T.rearrange("(c p) n -> p c n", p=P), loads_c)
            sp.wait_ge(zeros_done, 2)
            ez = E_[:, :, :, :].rearrange("p a b c -> p (a b c)")
            zdst = scratch.rearrange("k r n -> (k r) n").rearrange("(a p) n -> p a n", p=P)
            for a in range(2):
                sp.dma_start(zdst[:, 2 * a:2 * a + 2, :], ez.rearrange("p (a n) -> p a n", a=2)).then_inc(scratch_zero, 16)

            def body(j, main, post, late, ahead):
                if ahead:
                    wait(sp, g_full, 4 * j + 4)
                    load(xg[:], xT[bass.ds(j + 1, 1)].rearrange("a (c p) t -> p (a c) t", p=P), xg_in)
                if not (post or late):
                    sp.wait_ge(scratch_zero, 32)
                if post:
                    wait(sp, v_full, 4 * j - 4)
                    load(xv[:, :, W:W + T], xT[bass.ds(j - 1, 1)].rearrange("a (c p) t -> p (a c) t", p=P), xv_in)
                if late:
                    wait(sp, norm_done, 8 * j - 8)
                    load(out[bass.ds(j - 2, 1)].rearrange("a (n p) c -> p (a n) c", p=P), xt[:], stored)
                if post:
                    wait(sp, stored, 16 * j - 16)
                    load(xt[:], x_rows[bass.ds(j - 1, 1)].rearrange("a (n p) c -> p (a n) c", p=P), xt_in)
                    sp.wait_ge(scratch_zero, 32)
                    wait(sp, pv_done, 16 * j - 16)
                    for tb in range(TB):
                        wait(sp, exp_done, 4 * j - 4 + tb + 1)
                        for half in range(2):
                            src = E_[64 * half:64 * half + 64, tb, :, :]
                            dst = bass.AP(tensor=scratch.tensor, offset=(2 * tb + half) * W * NH * BAND + 1,
                                          ap=[[NH * BAND + 1, W], [BAND, NH], [1, W]])
                            sp.dma_start(dst, src).then_inc(skew_out[tb], 16)
                    for n in range(TB * HG):
                        tb, hg = n // HG, n % HG
                        if hg == 0:
                            sp.wait_ge(scratch_zero, 32)
                            wait(sp, skew_out[tb], 32 * j)
                        wait(sp, pt_full, 16 * j - 16 + max(n - 3, 0))
                        src = scratch[2 * tb:2 * tb + 2, :, hg * HPG * BAND:(hg + 1) * HPG * BAND]
                        load(band[:, n % 4, :, :].rearrange("p h n -> p (h n)"),
                             src.rearrange("k r n -> (k r) n"), band_in[n % 4])

            batches(sp, body)
            sp.wait_ge(stored, 16 * B)

        @block.scalar
        def _(act):
            act.wait_ge(loads_b, 80)
            nc.scalar.mul(dbias[:, 1:2], dbias[:, 0:1], 0.5).then_inc(prep_done, 1)
            act.wait_ge(loads_c, 32)
            nc.scalar.activation(wtmp, w1[:].rearrange("p a b -> p (a b)"), ACT.Abs,
                                 accum_out=tern[:, 0:1]).then_inc(tern_sum, 1)
            act.wait_ge(tern_sum, 1)
            nc.scalar.activation(wtmp, w2[:].rearrange("p a b -> p (a b)"), ACT.Abs,
                                 accum_out=tern[:, 1:2]).then_inc(tern_sum, 1)

            def gelu(j, step):
                for w, n in GELUS:
                    if w != step:
                        continue
                    v = ring[:, w % SLOTS:w % SLOTS + n, :, first_token(w):T].rearrange("p s g t -> p (s g) t")
                    if w in POOL_SLOTS:
                        wait(act, diff_pool, NP_ * j + on_pool(w + n))
                        nc.scalar.activation(v, v, ACT.Gelu, bias=posb[:, w:w + 1]).then_inc(gelu_done, 1)
                    else:
                        wait(act, diff_dve, ND * j + on_vector(w + n))
                        nc.scalar.activation(v, v, ACT.Gelu).then_inc(gelu_done, 1)

            def hidden_gelu(j, n):
                wait(act, h_full, 8 * j + n + 1)
                if n == 4:
                    wait(act, f2_full, 4 * j + 2)
                if n == 0:
                    wait(act, f2_full, 4 * j)
                for i in range(2):
                    f = 2 * (n % 4) + i
                    ins = nc.scalar.activation(hT[:, f, :], ms_ps[(n + 1) % 2][:, i * HALF:(i + 1) * HALF],
                                               ACT.Gelu, bias=b1_sb[:, f:f + 1])
                ins.then_inc(h_gelu, 1)

            def body(j, main, post, late, ahead):
                for step in range(W):
                    if main:
                        gelu(j, step)
                    if post and step == TANH:
                        wait(act, lt_evac, 16 * j)
                        nc.scalar.activation(L[:, :, 1, :, :], L[:, :, 1, :, :], ACT.Tanh,
                                             bias=dbias[:, 1:2], scale=0.5).then_inc(tanh_done, 1)
                    if post and step == EXP:
                        wait(act, sub_done, 1 * j)
                        for tb in range(TB):
                            e = E_[:, tb, :, :].rearrange("p b c -> p (b c)")
                            nc.scalar.activation(e, e, ACT.Exp).then_inc(exp_done, 1)
                    for n in range(8):
                        at = HIDDEN0 + 1 + n + n // 2 if n < 4 else HIDDEN1 + 1 + n - 4
                        if (b := due(j, step, at, post, late)) is not None:
                            hidden_gelu(b, n)

            act.wait_ge(prep_done, 5)
            act.wait_ge(pos_made, 2)
            batches(act, body)

        def strain_operands(w):
            k, lo = W - 1 - w, first_token(w)
            return ring[:, w % SLOTS, :, lo:T], G[:, :, W + lo - k:W + T - k], G[:, :, W + lo:W + T]

        @block.gpsimd
        def _(pool):
            nc.gpsimd.memset(ones[:], 1.0).then_inc(tern_step, 1)
            pool.wait_ge(tern_step, 1)
            nc.gpsimd.affine_select(out=ident[:], in_=ones[:], pattern=[[-1, P]], compare_op=ALU.is_equal, fill=0.0,
                                    base=0, channel_multiplier=1).then_inc(prep_done, 1)
            nc.gpsimd.memset(mask[:], 0.0).then_inc(tern_step, 1)
            pool.wait_ge(tern_step, 2)
            nc.gpsimd.affine_select(out=mask[:], in_=mask[:], pattern=[[1, W]], compare_op=ALU.is_ge, fill=MASKED,
                                    base=1 - W, channel_multiplier=1).then_inc(prep_done, 1)
            nc.gpsimd.memset(minus_half[:], -0.5).then_inc(prep_done, 1)
            nc.gpsimd.memset(V1[:, :, :, HS:VW], 1.0).then_inc(prep_done, 1)
            pool.wait_ge(prep_done, 5)

            def strain(j, w):
                if w in POOL_SLOTS:
                    wait(pool, g_evac, 4 * j + 4)
                    wait(pool, slot_used, 64 * j + w - SLOTS + 1)
                    out_w, past, now = strain_operands(w)
                    nc.gpsimd.tensor_tensor(out_w, past, now, ALU.subtract).then_inc(diff_pool, 1)

            def rstd_of(j, n):
                wait(pool, ve_done, 8 * j + n + 1)
                nc.gpsimd.tensor_tensor(rstd[:, n:n + 1], ve[:, n:n + 1], minus_half[:], ALU.pow).then_inc(rstd_done, 1)

            def add_b2(j, half):
                wait(pool, xt_full, 2 * j + half + 1)
                for n in range(2):
                    ins = nc.gpsimd.tensor_tensor(xt[:, 2 * half + n, :], xt[:, 2 * half + n, :], b2_sb[:], ALU.add)
                ins.then_inc(b2_added, 1)

            def body(j, main, post, late, ahead):
                for step in range(W):
                    if main and step < W - LEAD:
                        strain(j, step + LEAD)
                    if ahead and step >= W - LEAD:
                        strain(j + 1, step + LEAD - W)
                    if post and step == MASK:
                        wait(pool, logit_done, 1 * j)
                        nc.gpsimd.tensor_tensor(E_[:, 0, :, :], E_[:, 0, :, :],
                                                mask[:].unsqueeze(1).to_broadcast([P, NH, W]),
                                                ALU.add).then_inc(masked, 1)
                    for tb in range(TB):
                        if post and step == BANDS + 12 + 5 * tb:
                            rstd_of(j - 1, tb)
                    for half, turn, feed in ((0, TURN0, FEED0), (1, TURN1, FEED1)):
                        if (b := due(j, step, turn + 3, post, late)) is not None:
                            add_b2(b, half)
                        for n in range(2):
                            if (b := due(j, step, feed + 4 + n, post, late)) is not None:
                                rstd_of(b, TB + 2 * half + n)

            pool.wait_ge(pos_made, 2)
            for w in range(LEAD):
                strain(0, w)
            batches(pool, body)

        @block.vector
        def _(dve):
            for z in (ring[0:64, 1, 0, 0:P], ring[0:16, 1, 1, 0:P], wlog[:]):
                ins = nc.vector.memset(z, 0.0)
            ins.then_inc(zeros_done, 1)
            nc.vector.memset(E_[:], 0.0).then_inc(zeros_done, 1)
            for z in (G[:, :, 0:W], xv[:, :, 0:W], lg_ps[0][:], lg_ps[1][:]):
                ins = nc.vector.memset(z, 0.0)
            ins.then_inc(zeros_done, 1)

            dve.wait_ge(wc_made, 1)
            for c in range(CC):
                ins = nc.vector.tensor_copy(Wc[:, c, :, :].rearrange("p g n -> p (g n)"), ms_ps[c][:])
            ins.then_inc(wc_made, 1)
            dve.wait_ge(pos_made, 1)
            nc.vector.tensor_scalar(posb[:], lt_ps[:, 0:W], sbias[:, 0:1], None, ALU.add).then_inc(pos_made, 1)

            def ternary():
                def step(ins):
                    steps[0] += 1
                    ins.then_inc(tern_step, 1)
                    dve.wait_ge(tern_step, steps[0])

                steps = [2]
                dve.wait_ge(tern_tot, 1)
                step(nc.vector.tensor_scalar(tern[:, 2:4], o_ps[:, 0:2], 1.0 / (FF * C), 1e-8, ALU.mult, ALU.max))
                step(nc.vector.reciprocal(tern[:, 4:6], tern[:, 2:4]))
                for n, wt in enumerate((w1, w2)):
                    v = wt[:].rearrange("p a b -> p (a b)")
                    r = wtmp
                    step(nc.vector.tensor_scalar(r, v, tern[:, 4 + n:5 + n], MAGIC, ALU.mult, ALU.add))
                    step(nc.vector.tensor_scalar(r, r, MAGIC, 1.0, ALU.subtract, ALU.min))
                    step(nc.vector.scalar_tensor_tensor(out=r, in0=r, scalar=-1.0, in1=v, op0=ALU.max, op1=ALU.subtract))
                    step(nc.vector.tensor_tensor(v, v, r, ALU.add))
                nc.vector.tensor_copy(tern[:, 6:7], tern[:, 4:5]).then_inc(tern_done, 1)

            def g_copy(j):
                for hg in range(HG):
                    wait(dve, g_full, 4 * j + hg + 1)
                    if hg == 0:
                        wait(dve, diff_pool, NP_ * j)
                        wait(dve, diff_dve, ND * j)
                    nc.vector.tensor_copy(G[:, hg, W:W + T], g_ps[hg][:]).then_inc(g_evac, 1)
                wait(dve, g_evac, 4 * j + 4)

            def strain(j, w):
                if w in POOL_SLOTS:
                    return
                wait(dve, slot_used, 64 * j + w - SLOTS + 1)
                out_w, past, now = strain_operands(w)
                nc.vector.scalar_tensor_tensor(out=out_w, in0=past, scalar=posb[:, w:w + 1], in1=now, op0=ALU.add,
                                               op1=ALU.subtract).then_inc(diff_dve, 1)

            def logits_out(j, m):
                wait(dve, slot_used, 64 * j + 4 * m + 4)
                wait(dve, lt_full, 16 * j + m - 1)
                nc.vector.tensor_copy(lg_sb[:, m % 2, :], lg_ps[m % 2][:]).then_inc(lg_evac, 1)

            def logits_turned(j, m):
                wait(dve, lt_full, 16 * j + m + 1)
                if m == 0:
                    wait(dve, logit_done, 1 * j)
                nc.vector.tensor_copy(L[:, :, :, 4 * m:4 * m + 4, :].rearrange("p g y w h -> p g y (w h)"),
                                      lt_ps[:].rearrange("p (g y r) -> p g y r", g=TB * HG, y=2)).then_inc(lt_evac, 1)

            e_rows = E_[:].rearrange("p a b c -> p (a b) c")

            def combine(j):
                wait(dve, tanh_done, 1 * j)
                for tb in range(TB):
                    wait(dve, skew_out[tb], 32 * j - 32)
                for h in range(HPG):
                    ins = nc.vector.scalar_tensor_tensor(
                        out=E_[:].rearrange("p a (g h) w -> p (a g) h w", h=HPG)[:, :, h, :], in0=L[:, :, 1, :, h],
                        scalar=-5.0, in1=L[:, :, 0, :, h], op0=ALU.mult, op1=ALU.add)
                ins.then_inc(logit_done, 1)

            def maximum(j):
                wait(dve, masked, 1 * j)
                nc.vector.tensor_reduce(mx[:], e_rows, AX_X, ALU.max).then_inc(max_done, 1)

            def less_maximum(j):
                wait(dve, max_done, 1 * j)
                nc.vector.tensor_tensor(e_rows, e_rows, mx[:].unsqueeze(2).to_broadcast([P, TB * NH, W]),
                                        ALU.subtract).then_inc(sub_done, 1)

            def values_out(j, n):
                wait(dve, v_full, 4 * j + n + 1)
                nc.vector.tensor_copy(V1[:, 2 * n:2 * n + 2, :, 0:HS].rearrange("p k h d -> p (k h) d"),
                                      ms_ps[n % 2][:].rearrange("p (k d) -> p k d", d=HS)).then_inc(v_evac, 1)

            def band_turned(j, n):
                wait(dve, pt_full, 16 * j + n + 1)
                wait(dve, pv_done, 16 * j + max(n - 1, 0))
                nc.vector.tensor_copy(pt_sb[:, n % 2, :, :].rearrange("p h t -> p (h t)"),
                                      pt_ps[n % 2][:]).then_inc(pt_evac, 1)

            def attention_out(j, tb):
                o = o_ps[:, 0:NH * VW].rearrange("p (h d) -> p h d", d=VW)
                wait(dve, pv_done, 16 * j + 4 * tb + 4)
                nc.vector.reciprocal(rden[:, tb % 2, :], o[:, :, HS]).then_inc(den_done, 1)
                wait(dve, den_done, 4 * j + tb + 1)
                wait(dve, ot_full, 4 * j + max(tb - 1, 0))
                nc.vector.tensor_tensor(o_sb[:, tb % 2, :].rearrange("p (h d) -> p h d", d=HS), o[:, :, 0:HS],
                                        rden[:, tb % 2, :].unsqueeze(2).to_broadcast([P, NH, HS]),
                                        ALU.mult).then_inc(o_norm, 1)

            def attention_turned(j, tb):
                wait(dve, ot_full, 4 * j + tb + 1)
                wait(dve, cp_full, 4 * j + max(tb - 1, 0))
                nc.vector.tensor_copy(oT_sb[:, tb % 2, :, :].rearrange("p c t -> p (c t)"),
                                      ms_ps[0][:, 0:CC * P]).then_inc(ot_evac, 1)

            def sum_and_stats(j, n, arrived, value):
                row = xt[:, n % TB, :]
                product = ms_ps[1 if n < TB else (n + 1) % 2][:, 0:C]
                wait(dve, arrived, value)
                nc.vector.tensor_tensor(row, product, row, ALU.add).then_inc(sum_done, 1)
                wait(dve, sum_done, 8 * j + n + 1)
                nc.vector.bn_stats(stats[:, n, :], row).then_inc(stat_done, 1)
                dve.wait_ge(zeros_done, 3)
                wait(dve, stat_done, 8 * j + n + 1)
                nc.vector.bn_aggr(mv[:, n, :], stats[:, n, :]).then_inc(aggr_done, 1)
                wait(dve, aggr_done, 8 * j + n + 1)
                nc.vector.tensor_scalar(ve[:, n:n + 1], mv[:, n, 1:2], EPS, None, ALU.add).then_inc(ve_done, 1)

            def normalise(j, n):
                wait(dve, rstd_done, 8 * j + n + 1)
                nc.vector.tensor_scalar(xt[:, n % TB, :], xt[:, n % TB, :], mv[:, n, 0:1], rstd[:, n:n + 1],
                                        ALU.subtract, ALU.mult).then_inc(norm_done, 1)

            def tokens_turned(j, half):
                wait(dve, xt_full, 2 * j + half + 1)
                if half:
                    wait(dve, h_full, 8 * j + 4)
                else:
                    wait(dve, h_full, 8 * j)
                nc.vector.tensor_copy(x1T[:].rearrange("p c (n t) -> p n c t", n=2),
                                      ms_ps[0][:].rearrange("p (n c t) -> p n c t", n=2, c=CC)).then_inc(xt_evac, 1)

            def body(j, main, post, late, ahead):
                for step in range(W):
                    m = step // 4
                    if ahead and step == W - LEAD:
                        g_copy(j + 1)
                    if post and step == 0:
                        logits_out(j - 1, MS - 1)
                    if main and step % 4 == 0 and m:
                        logits_out(j, m - 1)
                    if post and step == COMBINE:
                        combine(j)
                    if post and step == 3:
                        logits_turned(j - 1, MS - 1)
                    if main and step % 4 == 3 and m:
                        logits_turned(j, m - 1)
                    for n in range(4):
                        if post and step == VALUES + 2 + 2 * n:
                            values_out(j - 1, n)
                    for tb in range(TB):
                        at = step - BANDS - 5 * tb
                        if post and 1 <= at < 5:
                            band_turned(j - 1, 4 * tb + at - 1)
                        if post and at == 6:
                            attention_out(j - 1, tb)
                        if post and at == 8:
                            attention_turned(j - 1, tb)
                    for half, turn in ((0, TURN0 + 1), (1, TURN1 + 2)):
                        if (b := due(j, step, turn, post, late)) is not None:
                            tokens_turned(b, half)
                    if main and step < W - LEAD:
                        strain(j, step + LEAD)
                    if ahead and step >= W - LEAD:
                        strain(j + 1, step + LEAD - W)
                    if post and step == MAXIMUM:
                        maximum(j)
                    if post and step == MAXIMUM + 2:
                        less_maximum(j)
                    for tb in range(TB):
                        at = step - BANDS - 5 * tb
                        if post and at == 11:
                            wait(dve, xt_in, 16 * j)
                            sum_and_stats(j - 1, tb, cp_full, 4 * j - 4 + tb + 1)
                        if post and at == 14:
                            normalise(j - 1, tb)
                    for n in range(TB):
                        feed = (FEED0 if n < 2 else FEED1) + n % 2
                        if (b := due(j, step, feed + 2, post, late)) is not None:
                            wait(dve, b2_added, 2 * b + n // 2 + 1)
                            sum_and_stats(b, TB + n, f2_full, 4 * b + n + 1)
                        if (b := due(j, step, feed + 6, post, late)) is not None:
                            normalise(b, TB + n)
                    if not (post or late) and step == 24:
                        ternary()
                        dve.wait_ge(scratch_zero, 32)

            g_copy(0)
            for w in range(LEAD):
                strain(0, w)
            batches(dve, body)

        @block.tensor
        def _(pe):
            pe.wait_ge(loads_a, 16 * (2 + 5 * HPG))
            pe.wait_ge(zeros_done, 3)
            for c in range(CC):
                for hg in range(HG):
                    ins = nc.tensor.matmul(ms_ps[c][:, hg * P:(hg + 1) * P], wd[:, hg, c * P:(c + 1) * P], bdiag,
                                           start=True, stop=True)
            ins.then_inc(wc_made, 1)
            nc.tensor.matmul(lt_ps[:, 0:W], ppw.rearrange("p h f -> p (h f)"), rel, start=True,
                             stop=True).then_inc(pos_made, 1)
            pe.wait_ge(wc_made, 2)

            def project_g(j, hg):
                if hg == 0:
                    wait(pe, xg_in, 16 * j + 16)
                    wait(pe, pt_evac, 16 * j - 16)
                if hg == 2:
                    wait(pe, o_norm, 4 * j - 4)
                if hg == 3:
                    wait(pe, sum_done, 8 * j - 8 - 3)
                for c in range(CC):
                    ins = nc.tensor.matmul(g_ps[hg][:], Wc[:, c, hg, :], xg[:, c, :], start=(c == 0), stop=(c == CC - 1))
                ins.then_inc(g_full, 1)

            def slot_logits(j, w):
                wait(pe, gelu_done, NG * j + gelus_through(w))
                m, s = w // 4, w % 4
                if s == 0:
                    wait(pe, lg_evac, 16 * j + m - 1)
                lo = first_token(w)
                for hg in range(HG):
                    ins = nc.tensor.matmul(lg_ps[m % 2][32 * hg:32 * hg + 32, lo:T], wlog[:, s, :],
                                           ring[:, w % SLOTS, hg, lo:T], start=(s == 0), stop=(s == 3))
                ins.then_inc(slot_used, 1)

            def turn_logits(j, m):
                wait(pe, lg_evac, 16 * j + m + 1)
                wait(pe, lt_evac, 16 * j + m)
                for tb in range(TB):
                    ins = nc.tensor.transpose(lt_ps[:, tb * P:(tb + 1) * P], lg_sb[:, m % 2, tb * P:(tb + 1) * P], ident[:])
                ins.then_inc(lt_full, 1)

            def values(j, n):
                if n == 0:
                    wait(pe, xv_in, 16 * j + 16)
                if n < 2:
                    wait(pe, sum_done, 8 * j)
                else:
                    wait(pe, v_evac, 4 * j + n - 1)
                for i in range(2):
                    kb = 2 * n + i
                    for c in range(CC):
                        ins = nc.tensor.matmul(ms_ps[n % 2][:, i * C:(i + 1) * C], xv[:, c, W * kb:W * kb + P],
                                               wv[:, c, :], start=(c == 0), stop=(c == CC - 1))
                ins.then_inc(v_full, 1)

            def turn_band(j, n, main):
                wait(pe, band_in[n % 4], 64 * j + 16 * (n // 4) + 16)
                if n < 2:
                    wait(pe, g_evac, 4 * j + 4 + 4 * main)
                else:
                    wait(pe, pt_evac, 16 * j + n - 1)
                for h in range(HPG):
                    ins = nc.tensor.transpose(pt_ps[n % 2][:, h * P:(h + 1) * P], band[:, n % 4, h, :], ident[:])
                ins.then_inc(pt_full, 1)

            def weigh_values(j, n):
                tb, hg = n // HG, n % HG
                wait(pe, pt_evac, 16 * j + n + 1)
                if n == 0:
                    wait(pe, v_evac, 4 * j + 4)
                if hg == 0:
                    wait(pe, o_norm, 4 * j + tb)
                for h in range(HPG):
                    for half in range(2):
                        col = (hg * HPG + h) * VW
                        ins = nc.tensor.matmul(o_ps[64 * half:64 * half + 64, col:col + VW],
                                               pt_sb[:, n % 2, h, 64 * half:64 * half + 64],
                                               V1[:, 2 * tb + half, hg * HPG + h, :], start=True, stop=True)
                ins.then_inc(pv_done, 1)

            def turn_attention(j, tb):
                wait(pe, o_norm, 4 * j + tb + 1)
                if tb == 0:
                    wait(pe, v_evac, 4 * j + 4)
                for c in range(CC):
                    ins = nc.tensor.transpose(ms_ps[0][:, c * P:(c + 1) * P], o_sb[:, tb % 2, c * P:(c + 1) * P], ident[:])
                ins.then_inc(ot_full, 1)

            def project_attention(j, tb):
                wait(pe, ot_evac, 4 * j + tb + 1)
                wait(pe, sum_done, 8 * j + tb)
                for c in range(CC):
                    ins = nc.tensor.matmul(ms_ps[1][:, 0:C], oT_sb[:, tb % 2, c, :], cp[:, c, :],
                                           start=(c == 0), stop=(c == CC - 1))
                ins.then_inc(cp_full, 1)

            def turn_tokens(j, half):
                wait(pe, norm_done, 8 * j + 2 * half + 2)
                if half == 0:
                    wait(pe, ot_evac, 4 * j + 4)
                else:
                    wait(pe, sum_done, 8 * j + 6)
                for n in range(2):
                    for c in range(CC):
                        ins = nc.tensor.transpose(ms_ps[0][:, (n * CC + c) * P:(n * CC + c + 1) * P],
                                                  xt[:, 2 * half + n, c * P:(c + 1) * P], ident[:])
                ins.then_inc(xt_full, 1)

            def hidden(j, n, ahead=False):
                if n % 4 == 0:
                    wait(pe, xt_evac, 2 * j + n // 4 + 1)
                    wait(pe, sum_done, 8 * j + (4 if n == 0 else 6))
                if n == 4 and ahead:
                    wait(pe, g_evac, 4 * j + 12)
                if n % 4 >= 2:
                    wait(pe, h_gelu, 8 * j + n - 1)
                for i in range(2):
                    f = 2 * (n % 4) + i
                    for c in range(CC):
                        ins = nc.tensor.matmul(ms_ps[(n + 1) % 2][:, i * HALF:(i + 1) * HALF],
                                               w1[:, c, f * P:(f + 1) * P], x1T[:, c, :],
                                               start=(c == 0), stop=(c == CC - 1))
                ins.then_inc(h_full, 1)

            def feed_out(j, n):
                wait(pe, h_gelu, 8 * j + 4 * (n // 2) + 4)
                for f in range(FC):
                    ins = nc.tensor.matmul(ms_ps[(n + 1) % 2][:, 0:C], hT[:, f, (n % 2) * P:(n % 2 + 1) * P], w2[:, f, :],
                                           start=(f == 0), stop=(f == FC - 1))
                ins.then_inc(f2_full, 1)

            def body(j, main, post, late, ahead):
                for step in range(W):
                    for tb in range(TB):
                        at = step - BANDS - 5 * tb
                        if post and 0 <= at < 4:
                            turn_band(j - 1, 4 * tb + at, main)
                    if main:
                        slot_logits(j, step)
                    if post and step == 1:
                        turn_logits(j - 1, MS - 1)
                    if main and step % 4 == 1 and step > 4:
                        turn_logits(j, step // 4 - 1)
                    for n in range(4):
                        if post and step == VALUES + 2 * n:
                            values(j - 1, n)
                    for tb in range(TB):
                        at = step - BANDS - 5 * tb
                        if post and 2 <= at < 6:
                            weigh_values(j - 1, 4 * tb + at - 2)
                        if post and at == 7:
                            turn_attention(j - 1, tb)
                        if post and at == 9:
                            project_attention(j - 1, tb)
                    if post and step == TURN0:
                        turn_tokens(j - 1, 0)
                    for n in range(8):
                        at = HIDDEN0 + n + n // 2 if n < 4 else HIDDEN1 + n - 4
                        if (b := due(j, step, at, post, late)) is not None:
                            hidden(b, n, ahead)
                    for n in range(4):
                        if (b := due(j, step, (FEED0 if n < 2 else FEED1) + n % 2, post, late)) is not None:
                            feed_out(b, n)
                        if ahead and step == NEXT_G + n:
                            project_g(j + 1, n)
                    if post and step == TURN1:
                        turn_tokens(j - 1, 1)
                    if not (post or late) and step == 52:
                        pe.wait_ge(tern_done, 1)
                    if not (post or late) and step == 12:
                        pe.wait_ge(g_evac, HG)
                        pe.wait_ge(tern_sum, 2)
                        nc.tensor.matmul(o_ps[:, 0:2], ones[:], tern[:, 0:2], start=True, stop=True).then_inc(tern_tot, 1)

            for hg in range(HG):
                project_g(0, hg)
            pe.wait_ge(prep_done, 5)
            pe.wait_ge(loads_b, 80)
            batches(pe, body)


def kernel(**inputs):
    import numpy as np
    import concourse.bacc as bacc
    from concourse.bass_utils import run_bass_kernel_spmd

    x = np.asarray(inputs["L0_attn_x"])
    def t(name):
        return np.ascontiguousarray(np.asarray(inputs[name]).T)

    data = {
        "xT": np.ascontiguousarray(x.transpose(0, 2, 1)),
        "x_rows": np.ascontiguousarray(x),
        "w_disp": np.ascontiguousarray(inputs["L0_attn_W_disp"]),
        "w_valT": t("L0_attn_W_val"),
        "relT": t("L0_attn_rel_pos_emb"),
        "strain_wT": t("L0_attn_strain_fused_w"),
        "strain_b": np.ascontiguousarray(inputs["L0_attn_strain_fused_b"]),
        "pos_wT": t("L0_attn_pos_proj_w"),
        "bond_w": np.ascontiguousarray(inputs["L0_attn_bond_out_w"]),
        "damage_w": np.ascontiguousarray(inputs["L0_attn_damage_out_w"]),
        "damage_b": np.ascontiguousarray(inputs["L0_attn_damage_out_b"]),
        "c_projT": t("L0_attn_c_proj_w"),
        "w1T": t("L0_ffn_W1"),
        "b1": np.ascontiguousarray(np.asarray(inputs["L0_ffn_b1"]).reshape(FC, P).T),
        "w2T": t("L0_ffn_W2"),
        "b2": np.ascontiguousarray(inputs["L0_ffn_b2"]),
    }
    nc = bacc.Bacc("TRN2", target_bir_lowering=False, num_devices=1)
    arrays = {f"in_{n}": a for n, a in data.items()}
    args = [nc.dram_tensor(f"in_{n}", a.shape, mybir.dt.from_np(a.dtype), kind="ExternalInput").ap()
            for n, a in data.items()]
    result = nc.dram_tensor("out_0", (B, T, C), F32, kind="ExternalOutput").ap()
    post_ln_block(nc, *args, result)
    r = run_bass_kernel_spmd(nc, [arrays], core_ids=[0])
    return r.results[0]["out_0"]
```

```python
import concourse.bass as bass
from concourse import mybir
from concourse.alu_op_type import AluOpType as ALU
from contextlib import ExitStack

ACT = mybir.ActivationFunctionType
AX_X = mybir.AxisListType.X
F32 = mybir.dt.float32

P = 128
B, T, C = 8, 512, 256
NH, HS, BD = 16, 16, 16
W = 64
FF = 4 * C
EPS = 1e-5
HPG = P // (2 * BD)
HG = NH // HPG
CC = C // P
TB = T // P
KB = T // W
MS = W // 4
SLOTS = 8
BAND = 2 * W
VW = HS + 1
FC = FF // P
HALF = 2 * P
GELU_LEAD = 2
LEAD = 6
OUT_AT = 0
TURN_AT = 1
TANH = 4
MASK = 10
EXP = 17
COMBINE = (6, 7, 8, 8)
MAXIMUM = (10, 11, 12, 15)
LESS = (11, 12, 14, 16)
VALUES = (14, 17, 18, 20)
BANDS = 22
STRIDE = 6
TURN_O = (32, 38, 44, 48)
PROJECT = (33, 39, 45, 49)
TURN = (46, 64)
HIDDEN = (48, 50, 51, 53, 66, 67, 68, 70)
FEED = (59, 62, 72, 74)
NEXT_G = (55, 56, 57, 57)
G_ORDER = (2, 3, 0, 1)
HIDDEN_BANK = (1, 0, 1, 0, 0, 1, 0, 1)
FEED_BANK = (1, 0, 0, 1)
SUM_LAG = 1
NORM_LAG = 3
HIDDEN_LAG = 1
MAGIC = 1.5 * 2.0 ** 23
MASKED = -1e30

VECTOR_SLOTS = (3, 6, 8, 9, 30, 33, 37, 39, 42, 45, 48, 51, 54, 56, 60, 63)
POOL_SLOTS = frozenset(range(W)) - frozenset(VECTOR_SLOTS)


def on_pool(w):
    return sum(1 for v in range(w) if v in POOL_SLOTS)


NP_ = on_pool(W)


def first_token(w):
    return W - 4 - 4 * (w // 4)


def post_ln_block(nc, xT, x_rows, w_disp, w_valT, relT, strain_wT, strain_b, pos_wT, bond_w, damage_w,
                  damage_b, c_projT, w1T, b1, w2T, b2, out):
    scratch = nc.dram_tensor("band_scratch", (KB, W, NH * BAND), F32, kind="Internal").ap()

    with ExitStack() as ctx:
        def sb(name, *shape):
            return ctx.enter_context(nc.sbuf_tensor(name, list(shape), F32))

        def sem(name):
            return ctx.enter_context(nc.semaphore(name))

        ring = sb("ring", P, SLOTS, HG, T)
        G = sb("G", P, HG, W + T)
        xg = sb("xg", P, CC, T)
        xv = sb("xv", P, CC, W + T)
        lg_sb = sb("lg_sb", P, 2, T)
        L = sb("L", P, TB * HG, 2, W, HPG)
        E_ = sb("E_", P, TB, NH, W)
        band = sb("band", P, 4, HPG, BAND)
        pt_sb = sb("pt_sb", P, 2, HPG, P)
        V1 = sb("V1", P, KB, NH, VW)
        o_sb = sb("o_sb", P, 2, C)
        oT_sb = sb("oT_sb", P, 2, CC, P)
        xt = sb("xt", P, TB, C)
        x1T = sb("x1T", P, CC, HALF)
        hT = sb("hT", P, FC, HALF)
        mx = sb("mx", P, TB * NH)
        rden = sb("rden", P, 2, NH)
        stats = sb("stats", P, 2 * TB, 6)
        mv = sb("mv", P, 2 * TB, 2)
        ve = sb("ve", P, 2 * TB)
        rstd = sb("rstd", P, 2 * TB)
        minus_half = sb("minus_half", P, 1)
        Wc = sb("Wc", P, CC, HG, P)
        wv = sb("wv", P, CC, C)
        cp = sb("cp", P, CC, C)
        w1 = sb("w1", P, CC, FF)
        w2 = sb("w2", P, FC, C)
        wlog = sb("wlog", P, 4, 32)
        ident = sb("ident", P, P)
        ones = sb("ones", P, P)
        mask = sb("mask", P, W)
        posb = sb("posb", P, W)
        sbias = sb("sbias", P, 1)
        dbias = sb("dbias", P, 2)
        b1_sb = sb("b1_sb", P, FC)
        b2_sb = sb("b2_sb", P, C)
        tern = sb("tern", P, 8)
        wd = ring[0:64, 0, 0:2, :].rearrange("p a b -> p (a b)").rearrange("p (g c) -> p g c", g=HG)
        bdiag = ring[0:64, 1, 0, 0:P]
        ppw = ring[0:16, 1, 1, 0:P].rearrange("p (h f) -> p h f", h=HPG)
        rel = ring[0:16, 1, 2, 0:W]
        wtmp = hT[:].rearrange("p a b -> p (a b)")

        def ps(name):
            return ctx.enter_context(nc.psum_tensor(name, [P, 512], F32))

        lg_ps = [ps("lg_ps0"), ps("lg_ps1")]
        lt_ps = ps("lt_ps")
        G_ps = ctx.enter_context(nc.psum_tensor("G_ps", [P, 2, T], F32))
        o_ps = ps("o_ps")
        ms_ps = [ps("ms_ps0"), ps("ms_ps1")]
        g_ps = [G_ps[:, 0, :], G_ps[:, 1, :], ms_ps[1][:], ms_ps[0][:]]

        loads_a, loads_b, loads_c = sem("loads_a"), sem("loads_b"), sem("loads_c")
        zeros_done, prep_done = sem("zeros_done"), sem("prep_done")
        wc_made, pos_made, tern_sum, tern_tot = sem("wc_made"), sem("pos_made"), sem("tern_sum"), sem("tern_tot")
        tern_step, tern_done = sem("tern_step"), sem("tern_done")
        scratch_zero = sem("scratch_zero")
        xg_in, xv_in, xt_in = sem("xg_in"), sem("xv_in"), sem("xt_in")
        g_full, g_evac = sem("g_full"), sem("g_evac")
        diff_dve, diff_pool = sem("diff_dve"), sem("diff_pool")
        gelu_done, slot_used = sem("gelu_done"), sem("slot_used")
        lg_evac = sem("lg_evac")
        lt_full, lt_evac = sem("lt_full"), sem("lt_evac")
        tanh_done, logit_done, masked = sem("tanh_done"), sem("logit_done"), sem("masked")
        max_done, sub_done, exp_done = sem("max_done"), sem("sub_done"), sem("exp_done")
        skew_out = [sem(f"skew_out{i}") for i in range(TB)]
        band_in = [sem(f"band_in{i}") for i in range(4)]
        pt_full, pt_evac, pv_done = sem("pt_full"), sem("pt_evac"), sem("pv_done")
        den_done, o_norm = sem("den_done"), sem("o_norm")
        v_full, v_evac = sem("v_full"), sem("v_evac")
        ot_full, ot_evac = sem("ot_full"), sem("ot_evac")
        cp_full, sum_done, stat_done = sem("cp_full"), sem("sum_done"), sem("stat_done")
        aggr_done, ve_done, rstd_done = sem("aggr_done"), sem("ve_done"), sem("rstd_done")
        norm_done = sem("norm_done")
        xt_full, xt_evac, b2_added = sem("xt_full"), sem("xt_evac"), sem("b2_added")
        h_full, h_gelu = sem("h_full"), sem("h_gelu")
        f2_full = sem("f2_full")
        stored = sem("stored")

        def wait(eng, s, n):
            if not isinstance(n, int) or n > 0:
                eng.wait_ge(s, n)

        def batches(eng, body):
            body(0, main=True, post=False, late=False, ahead=True)
            body(1, main=True, post=True, late=False, ahead=True)
            with eng.Fori(2, B - 1) as j:
                body(j, main=True, post=True, late=True, ahead=True)
            body(B - 1, main=True, post=True, late=True, ahead=False)
            body(B, main=False, post=True, late=True, ahead=False)
            body(B + 1, main=False, post=False, late=True, ahead=False)

        def due(j, step, at, post, late):
            if post and step == at:
                return j - 1
            if late and step == at - W:
                return j - 2
            return None

        block = ctx.enter_context(nc.Block())

        @block.sync
        def _(sp):
            def load(dst, src, s):
                sp.dma_start(dst, src).then_inc(s, 16)

            load(wd, w_disp.rearrange("(g p) c -> p g c", p=64), loads_a)
            load(xg[:], xT[0].rearrange("(c p) t -> p c t", p=P), xg_in)
            load(rel, relT, loads_a)
            sp.wait_ge(zeros_done, 1)
            for h in range(HPG):
                load(bdiag[16 * h:16 * h + 16, 32 * h:32 * h + 32], strain_wT, loads_a)
                load(ppw[:, h, 0:16], pos_wT, loads_a)
                load(sbias[32 * h:32 * h + 32, :], strain_b.rearrange("(f a) -> f a", a=1), loads_a)
                for kind, src in ((0, bond_w), (1, damage_w)):
                    row = 32 * h + 16 * kind
                    dst = bass.AP(tensor=wlog[:].tensor, offset=row * 128 + 16 * kind + h, ap=[[128, 16], [36, 4], [1, 1]])
                    with nc.allow_non_contiguous_dma(reason="64 weights, once"):
                        load(dst, bass.AP(tensor=src.tensor, offset=0, ap=[[1, 16], [0, 4], [1, 1]]), loads_a)
            load(dbias[:, 0:1], damage_b.partition_broadcast(P), loads_b)
            load(b2_sb[:], b2.partition_broadcast(P), loads_b)
            load(b1_sb[:], b1, loads_b)
            load(wv[:], w_valT.rearrange("(c p) n -> p c n", p=P), loads_b)
            load(cp[:], c_projT.rearrange("(c p) n -> p c n", p=P), loads_b)
            load(w1[:], w1T.rearrange("(c p) n -> p c n", p=P), loads_c)
            load(w2[:], w2T.rearrange("(c p) n -> p c n", p=P), loads_c)
            sp.wait_ge(zeros_done, 2)
            ez = E_[:, :, :, :].rearrange("p a b c -> p (a b c)")
            zdst = scratch.rearrange("k r n -> (k r) n").rearrange("(a p) n -> p a n", p=P)
            for a in range(2):
                sp.dma_start(zdst[:, 2 * a:2 * a + 2, :], ez.rearrange("p (a n) -> p a n", a=2)).then_inc(scratch_zero, 16)

            def skew(j, tb):
                wait(sp, exp_done, 4 * j - 4 + tb + 1)
                for half in range(2):
                    src = E_[64 * half:64 * half + 64, tb, :, :]
                    dst = bass.AP(tensor=scratch.tensor, offset=(2 * tb + half) * W * NH * BAND + 1,
                                  ap=[[NH * BAND + 1, W], [BAND, NH], [1, W]])
                    sp.dma_start(dst, src).then_inc(skew_out[tb], 16)

            def body(j, main, post, late, ahead):
                if ahead:
                    wait(sp, g_full, 4 * j + 4)
                    load(xg[:], xT[bass.ds(j + 1, 1)].rearrange("a (c p) t -> p (a c) t", p=P), xg_in)
                if not (post or late):
                    sp.wait_ge(scratch_zero, 32)
                if post:
                    wait(sp, v_full, 4 * j - 4)
                    load(xv[:, :, W:W + T], xT[bass.ds(j - 1, 1)].rearrange("a (c p) t -> p (a c) t", p=P), xv_in)
                if late:
                    wait(sp, norm_done, 8 * j - 8)
                    load(out[bass.ds(j - 2, 1)].rearrange("a (n p) c -> p (a n) c", p=P), xt[:], stored)
                if post:
                    wait(sp, stored, 16 * j - 16)
                    load(xt[:], x_rows[bass.ds(j - 1, 1)].rearrange("a (n p) c -> p (a n) c", p=P), xt_in)
                    sp.wait_ge(scratch_zero, 32)
                    wait(sp, pv_done, 16 * j - 16)
                    skew(j, 0)
                    for tb in range(TB):
                        if tb < TB - 1:
                            skew(j, tb + 1)
                        sp.wait_ge(scratch_zero, 32)
                        wait(sp, skew_out[tb], 32 * j)
                        for hg in range(HG):
                            n = HG * tb + hg
                            wait(sp, pt_full, 16 * j - 16 + max(n - 3, 0))
                            src = scratch[2 * tb:2 * tb + 2, :, hg * HPG * BAND:(hg + 1) * HPG * BAND]
                            load(band[:, n % 4, :, :].rearrange("p h n -> p (h n)"),
                                 src.rearrange("k r n -> (k r) n"), band_in[n % 4])

            batches(sp, body)
            sp.wait_ge(stored, 16 * B)

        @block.scalar
        def _(act):
            act.wait_ge(loads_b, 80)
            nc.scalar.mul(dbias[:, 1:2], dbias[:, 0:1], 0.5).then_inc(prep_done, 1)
            act.wait_ge(loads_c, 32)
            nc.scalar.activation(wtmp, w1[:].rearrange("p a b -> p (a b)"), ACT.Abs,
                                 accum_out=tern[:, 0:1]).then_inc(tern_sum, 1)
            act.wait_ge(tern_sum, 1)
            nc.scalar.activation(wtmp, w2[:].rearrange("p a b -> p (a b)"), ACT.Abs,
                                 accum_out=tern[:, 1:2]).then_inc(tern_sum, 1)

            def gelu(j, w):
                v = ring[:, w % SLOTS, :, first_token(w):T]
                wait(act, diff_pool, NP_ * j + on_pool(w + 1))
                wait(act, diff_dve, W * j + w + 1)
                nc.scalar.activation(v, v, ACT.Gelu, bias=posb[:, w:w + 1]).then_inc(gelu_done, 1)

            def logits_out(j, m):
                wait(act, slot_used, W * j + 4 * m + 4)
                wait(act, lt_full, 16 * j + m - 1)
                nc.scalar.copy(lg_sb[:, m % 2, :], lg_ps[m % 2][:]).then_inc(lg_evac, 1)

            def hidden_gelu(j, n):
                wait(act, h_full, 8 * j + n + 1)
                if n == 4:
                    wait(act, f2_full, 4 * j + 2)
                if n == 0:
                    wait(act, f2_full, 4 * j)
                for i in range(2):
                    f = 2 * (n % 4) + i
                    ins = nc.scalar.activation(hT[:, f, :], ms_ps[HIDDEN_BANK[n]][:, i * HALF:(i + 1) * HALF],
                                               ACT.Gelu, bias=b1_sb[:, f:f + 1])
                ins.then_inc(h_gelu, 1)

            def body(j, main, post, late, ahead):
                for step in range(W):
                    if main and step < W - GELU_LEAD:
                        gelu(j, step + GELU_LEAD)
                    if ahead and step >= W - GELU_LEAD:
                        gelu(j + 1, step + GELU_LEAD - W)
                    if post and step == OUT_AT:
                        logits_out(j - 1, MS - 1)
                    if main and step % 4 == OUT_AT and step >= 4:
                        logits_out(j, step // 4 - 1)
                    if post and step == TANH:
                        wait(act, lt_evac, 16 * j)
                        nc.scalar.activation(L[:, :, 1, :, :], L[:, :, 1, :, :], ACT.Tanh,
                                             bias=dbias[:, 1:2], scale=0.5).then_inc(tanh_done, 1)
                    if post and step == EXP:
                        for tb in range(TB):
                            wait(act, sub_done, TB * j - TB + tb + 1)
                            e = E_[:, tb, :, :].rearrange("p b c -> p (b c)")
                            nc.scalar.activation(e, e, ACT.Exp).then_inc(exp_done, 1)
                    for n in range(8):
                        if (b := due(j, step, HIDDEN[n] + HIDDEN_LAG, post, late)) is not None:
                            hidden_gelu(b, n)

            act.wait_ge(prep_done, 5)
            act.wait_ge(pos_made, 2)
            for w in range(GELU_LEAD):
                gelu(0, w)
            batches(act, body)

        def strain_operands(w, hg):
            k, lo = W - 1 - w, first_token(w)
            now = G[:, hg:hg + 2, W + lo:W + T] if hg else G_ps[:, :, lo:T]
            return ring[:, w % SLOTS, hg:hg + 2, lo:T], G[:, hg:hg + 2, W + lo - k:W + T - k], now

        @block.gpsimd
        def _(pool):
            nc.gpsimd.memset(ones[:], 1.0).then_inc(tern_step, 1)
            pool.wait_ge(tern_step, 1)
            nc.gpsimd.affine_select(out=ident[:], in_=ones[:], pattern=[[-1, P]], compare_op=ALU.is_equal, fill=0.0,
                                    base=0, channel_multiplier=1).then_inc(prep_done, 1)
            nc.gpsimd.memset(mask[:], 0.0).then_inc(tern_step, 1)
            pool.wait_ge(tern_step, 2)
            nc.gpsimd.affine_select(out=mask[:], in_=mask[:], pattern=[[1, W]], compare_op=ALU.is_ge, fill=MASKED,
                                    base=1 - W, channel_multiplier=1).then_inc(prep_done, 1)
            nc.gpsimd.memset(minus_half[:], -0.5).then_inc(prep_done, 1)
            nc.gpsimd.memset(V1[:, :, :, HS:VW], 1.0).then_inc(prep_done, 1)
            pool.wait_ge(prep_done, 5)

            def strain(j, w):
                if w in POOL_SLOTS:
                    wait(pool, g_evac, 4 * j + 4)
                    wait(pool, slot_used, 64 * j + w - SLOTS + 1)
                    out_w, past, now = strain_operands(w, 2)
                    nc.gpsimd.tensor_tensor(out_w, past, now, ALU.subtract).then_inc(diff_pool, 1)

            def rstd_of(j, n):
                wait(pool, ve_done, 8 * j + n + 1)
                nc.gpsimd.tensor_tensor(rstd[:, n:n + 1], ve[:, n:n + 1], minus_half[:], ALU.pow).then_inc(rstd_done, 1)

            def add_b2(j, half):
                wait(pool, xt_full, 2 * j + half + 1)
                for n in range(2):
                    ins = nc.gpsimd.tensor_tensor(xt[:, 2 * half + n, :], xt[:, 2 * half + n, :], b2_sb[:], ALU.add)
                ins.then_inc(b2_added, 1)

            def body(j, main, post, late, ahead):
                for step in range(W):
                    if main and step < W - LEAD:
                        strain(j, step + LEAD)
                    if ahead and step >= W - LEAD:
                        strain(j + 1, step + LEAD - W)
                    if post and step == MASK:
                        wait(pool, logit_done, HPG * j)
                        nc.gpsimd.tensor_tensor(E_[:, 0, :, :], E_[:, 0, :, :],
                                                mask[:].unsqueeze(1).to_broadcast([P, NH, W]),
                                                ALU.add).then_inc(masked, 1)
                    for tb in range(TB):
                        if post and step == PROJECT[tb] + SUM_LAG:
                            rstd_of(j - 1, tb)
                    for half in range(2):
                        if (b := due(j, step, TURN[half] + 1, post, late)) is not None:
                            add_b2(b, half)
                    for n in range(TB):
                        if (b := due(j, step, FEED[n] + 2 + SUM_LAG, post, late)) is not None:
                            rstd_of(b, TB + n)

            pool.wait_ge(pos_made, 2)
            for w in range(LEAD):
                strain(0, w)
            batches(pool, body)

        @block.vector
        def _(dve):
            for z in (ring[0:64, 1, 0, 0:P], ring[0:16, 1, 1, 0:P], wlog[:]):
                ins = nc.vector.memset(z, 0.0)
            ins.then_inc(zeros_done, 1)
            nc.vector.memset(E_[:], 0.0).then_inc(zeros_done, 1)
            for z in (G[:, :, 0:W], xv[:, :, 0:W], lg_ps[0][:], lg_ps[1][:]):
                ins = nc.vector.memset(z, 0.0)
            ins.then_inc(zeros_done, 1)

            dve.wait_ge(wc_made, 1)
            for c in range(CC):
                ins = nc.vector.tensor_copy(Wc[:, c, :, :].rearrange("p g n -> p (g n)"), ms_ps[c][:])
            ins.then_inc(wc_made, 1)
            dve.wait_ge(pos_made, 1)
            nc.vector.tensor_scalar(posb[:], lt_ps[:, 0:W], sbias[:, 0:1], None, ALU.add).then_inc(pos_made, 1)

            def ternary():
                def step(ins):
                    steps[0] += 1
                    ins.then_inc(tern_step, 1)
                    dve.wait_ge(tern_step, steps[0])

                steps = [2]
                dve.wait_ge(tern_tot, 1)
                step(nc.vector.tensor_scalar(tern[:, 2:4], o_ps[:, 0:2], 1.0 / (FF * C), 1e-8, ALU.mult, ALU.max))
                step(nc.vector.reciprocal(tern[:, 4:6], tern[:, 2:4]))
                for n, wt in enumerate((w1, w2)):
                    v = wt[:].rearrange("p a b -> p (a b)")
                    r = wtmp
                    step(nc.vector.tensor_scalar(r, v, tern[:, 4 + n:5 + n], MAGIC, ALU.mult, ALU.add))
                    step(nc.vector.tensor_scalar(r, r, MAGIC, 1.0, ALU.subtract, ALU.min))
                    step(nc.vector.scalar_tensor_tensor(out=r, in0=r, scalar=-1.0, in1=v, op0=ALU.max, op1=ALU.subtract))
                    step(nc.vector.tensor_tensor(v, v, r, ALU.add))
                nc.vector.tensor_copy(tern[:, 6:7], tern[:, 4:5]).then_inc(tern_done, 1)

            def g_copy(j):
                for n, hg in enumerate(G_ORDER):
                    wait(dve, g_full, 4 * j + n + 1)
                    if n == 0:
                        wait(dve, diff_pool, NP_ * j)
                        wait(dve, diff_dve, W * j)
                    nc.vector.tensor_copy(G[:, hg, W:W + T], g_ps[hg]).then_inc(g_evac, 1)
                wait(dve, g_evac, 4 * j + 4)

            def strain(j, w):
                wait(dve, slot_used, 64 * j + w - SLOTS + 1)
                for hg in (0,) if w in POOL_SLOTS else (0, 2):
                    out_w, past, now = strain_operands(w, hg)
                    ins = nc.vector.tensor_tensor(out_w, past, now, ALU.subtract)
                ins.then_inc(diff_dve, 1)

            def logits_turned(j, m):
                wait(dve, lt_full, 16 * j + m + 1)
                if m == 0:
                    wait(dve, logit_done, HPG * j)
                nc.vector.tensor_copy(L[:, :, :, 4 * m:4 * m + 4, :].rearrange("p g y w h -> p g y (w h)"),
                                      lt_ps[:].rearrange("p (g y r) -> p g y r", g=TB * HG, y=2)).then_inc(lt_evac, 1)

            def combine(j, h):
                if h == 0:
                    wait(dve, tanh_done, 1 * j)
                    for tb in range(TB):
                        wait(dve, skew_out[tb], 32 * j - 32)
                nc.vector.scalar_tensor_tensor(
                    out=E_[:].rearrange("p a (g h) w -> p (a g) h w", h=HPG)[:, :, h, :], in0=L[:, :, 1, :, h],
                    scalar=-5.0, in1=L[:, :, 0, :, h], op0=ALU.mult, op1=ALU.add).then_inc(logit_done, 1)

            def maximum(j, tb):
                wait(dve, masked if tb == 0 else logit_done, 1 * j if tb == 0 else HPG * j)
                nc.vector.tensor_reduce(mx[:, tb * NH:(tb + 1) * NH], E_[:, tb, :, :], AX_X, ALU.max).then_inc(max_done, 1)

            def less_maximum(j, tb):
                wait(dve, max_done, TB * j - TB + tb + 1)
                nc.vector.tensor_tensor(E_[:, tb, :, :], E_[:, tb, :, :],
                                        mx[:, tb * NH:(tb + 1) * NH].unsqueeze(2).to_broadcast([P, NH, W]),
                                        ALU.subtract).then_inc(sub_done, 1)

            def values_out(j, n):
                wait(dve, v_full, 4 * j + n + 1)
                nc.vector.tensor_copy(V1[:, 2 * n:2 * n + 2, :, 0:HS].rearrange("p k h d -> p (k h) d"),
                                      ms_ps[n % 2][:].rearrange("p (k d) -> p k d", d=HS)).then_inc(v_evac, 1)

            def band_turned(j, n):
                wait(dve, pt_full, 16 * j + n + 1)
                wait(dve, pv_done, 16 * j + max(n - 1, 0))
                nc.vector.tensor_copy(pt_sb[:, n % 2, :, :].rearrange("p h t -> p (h t)"),
                                      ms_ps[n % 2][:]).then_inc(pt_evac, 1)

            def attention_out(j, tb):
                o = o_ps[:, 0:NH * VW].rearrange("p (h d) -> p h d", d=VW)
                wait(dve, pv_done, 16 * j + 4 * tb + 4)
                nc.vector.reciprocal(rden[:, tb % 2, :], o[:, :, HS]).then_inc(den_done, 1)
                wait(dve, den_done, 4 * j + tb + 1)
                wait(dve, ot_full, 4 * j + max(tb - 1, 0))
                nc.vector.tensor_tensor(o_sb[:, tb % 2, :].rearrange("p (h d) -> p h d", d=HS), o[:, :, 0:HS],
                                        rden[:, tb % 2, :].unsqueeze(2).to_broadcast([P, NH, HS]),
                                        ALU.mult).then_inc(o_norm, 1)

            def attention_turned(j, tb):
                wait(dve, ot_full, 4 * j + tb + 1)
                wait(dve, cp_full, 4 * j + max(tb - 1, 0))
                nc.vector.tensor_copy(oT_sb[:, tb % 2, :, :].rearrange("p c t -> p (c t)"),
                                      ms_ps[0][:, 0:CC * P]).then_inc(ot_evac, 1)

            def sum_and_stats(j, n, arrived, value):
                row = xt[:, n % TB, :]
                product = ms_ps[1 if n < TB else FEED_BANK[n - TB]][:, 0:C]
                wait(dve, arrived, value)
                nc.vector.tensor_tensor(row, product, row, ALU.add).then_inc(sum_done, 1)
                wait(dve, sum_done, 8 * j + n + 1)
                nc.vector.bn_stats(stats[:, n, :], row).then_inc(stat_done, 1)
                dve.wait_ge(zeros_done, 3)
                wait(dve, stat_done, 8 * j + n + 1)
                nc.vector.bn_aggr(mv[:, n, :], stats[:, n, :]).then_inc(aggr_done, 1)
                wait(dve, aggr_done, 8 * j + n + 1)
                nc.vector.tensor_scalar(ve[:, n:n + 1], mv[:, n, 1:2], EPS, None, ALU.add).then_inc(ve_done, 1)

            def normalise(j, n):
                wait(dve, rstd_done, 8 * j + n + 1)
                nc.vector.tensor_scalar(xt[:, n % TB, :], xt[:, n % TB, :], mv[:, n, 0:1], rstd[:, n:n + 1],
                                        ALU.subtract, ALU.mult).then_inc(norm_done, 1)

            def tokens_turned(j, half):
                wait(dve, xt_full, 2 * j + half + 1)
                if half:
                    wait(dve, h_full, 8 * j + 4)
                else:
                    wait(dve, h_full, 8 * j)
                nc.vector.tensor_copy(x1T[:].rearrange("p c (n t) -> p n c t", n=2),
                                      ms_ps[half][:].rearrange("p (n c t) -> p n c t", n=2, c=CC)).then_inc(xt_evac, 1)

            def body(j, main, post, late, ahead):
                for step in range(W):
                    m = step // 4
                    if ahead and step == W - LEAD:
                        g_copy(j + 1)
                    for h in range(HPG):
                        if post and step == COMBINE[h]:
                            combine(j, h)
                    if post and step == 3:
                        logits_turned(j - 1, MS - 1)
                    if main and step == 8:
                        logits_turned(j, 0)
                    if main and step % 4 == 3 and m > 1:
                        logits_turned(j, m - 1)
                    for n in range(4):
                        if post and step == VALUES[n] + 1:
                            values_out(j - 1, n)
                    for tb in range(TB):
                        at = step - BANDS - STRIDE * tb
                        if post and 1 <= at < 5:
                            band_turned(j - 1, 4 * tb + at - 1)
                        if post and at == 6:
                            attention_out(j - 1, tb)
                        if post and step == TURN_O[tb] + 1:
                            attention_turned(j - 1, tb)
                    for half in range(2):
                        if (b := due(j, step, TURN[half] + 1, post, late)) is not None:
                            tokens_turned(b, half)
                    if main and step < W - LEAD:
                        strain(j, step + LEAD)
                    if ahead and step >= W - LEAD:
                        strain(j + 1, step + LEAD - W)
                    for tb in range(TB):
                        if post and step == MAXIMUM[tb]:
                            maximum(j, tb)
                        if post and step == LESS[tb]:
                            less_maximum(j, tb)
                    for tb in range(TB):
                        if post and step == PROJECT[tb] + SUM_LAG:
                            wait(dve, xt_in, 16 * j)
                            sum_and_stats(j - 1, tb, cp_full, 4 * j - 4 + tb + 1)
                        if post and step == PROJECT[tb] + NORM_LAG:
                            normalise(j - 1, tb)
                    for n in range(TB):
                        feed = FEED[n]
                        if (b := due(j, step, feed + 1 + SUM_LAG, post, late)) is not None:
                            wait(dve, b2_added, 2 * b + n // 2 + 1)
                            sum_and_stats(b, TB + n, f2_full, 4 * b + n + 1)
                        if (b := due(j, step, feed + 2 + NORM_LAG, post, late)) is not None:
                            normalise(b, TB + n)
                    if not (post or late) and step == 24:
                        ternary()
                        dve.wait_ge(scratch_zero, 32)

            g_copy(0)
            for w in range(LEAD):
                strain(0, w)
            batches(dve, body)

        @block.tensor
        def _(pe):
            pe.wait_ge(loads_a, 16 * (2 + 5 * HPG))
            pe.wait_ge(zeros_done, 3)
            for c in range(CC):
                for hg in range(HG):
                    ins = nc.tensor.matmul(ms_ps[c][:, hg * P:(hg + 1) * P], wd[:, hg, c * P:(c + 1) * P], bdiag,
                                           start=True, stop=True)
            ins.then_inc(wc_made, 1)
            nc.tensor.matmul(lt_ps[:, 0:W], ppw.rearrange("p h f -> p (h f)"), rel, start=True,
                             stop=True).then_inc(pos_made, 1)
            pe.wait_ge(wc_made, 2)

            def project_g(j, hg):
                if hg == G_ORDER[0]:
                    wait(pe, xg_in, 16 * j + 16)
                if hg < 2:
                    wait(pe, diff_dve, W * j)
                else:
                    wait(pe, g_evac, 4 * j)
                    wait(pe, h_gelu, 8 * j - 16 + 3 + (hg - 2))
                for c in range(CC):
                    ins = nc.tensor.matmul(g_ps[hg], Wc[:, c, hg, :], xg[:, c, :], start=(c == 0), stop=(c == CC - 1))
                ins.then_inc(g_full, 1)

            def slot_logits(j, w):
                wait(pe, gelu_done, W * j + w + 1)
                m, s = w // 4, w % 4
                if s == 0:
                    wait(pe, lg_evac, 16 * j + m - 1)
                lo = first_token(w)
                for hg in range(HG):
                    ins = nc.tensor.matmul(lg_ps[m % 2][32 * hg:32 * hg + 32, lo:T], wlog[:, s, :],
                                           ring[:, w % SLOTS, hg, lo:T], start=(s == 0), stop=(s == 3))
                ins.then_inc(slot_used, 1)

            def turn_logits(j, m):
                wait(pe, lg_evac, 16 * j + m + 1)
                wait(pe, lt_evac, 16 * j + m)
                for tb in range(TB):
                    ins = nc.tensor.transpose(lt_ps[:, tb * P:(tb + 1) * P], lg_sb[:, m % 2, tb * P:(tb + 1) * P], ident[:])
                ins.then_inc(lt_full, 1)

            def values(j, n):
                if n == 0:
                    wait(pe, xv_in, 16 * j + 16)
                if n < 2:
                    wait(pe, sum_done, 8 * j - 1 + n)
                else:
                    wait(pe, v_evac, 4 * j + n - 1)
                for i in range(2):
                    kb = 2 * n + i
                    for c in range(CC):
                        ins = nc.tensor.matmul(ms_ps[n % 2][:, i * C:(i + 1) * C], xv[:, c, W * kb:W * kb + P],
                                               wv[:, c, :], start=(c == 0), stop=(c == CC - 1))
                ins.then_inc(v_full, 1)

            def turn_band(j, n):
                tb, hg = n // HG, n % HG
                wait(pe, band_in[n % 4], 64 * j + 16 * (n // 4) + 16)
                if n < 2:
                    wait(pe, v_evac, 4 * j + 3 + n)
                elif hg == 0 and tb >= 2:
                    wait(pe, ot_evac, 4 * j + tb - 1)
                elif hg == 1 and tb >= 2:
                    wait(pe, sum_done, 8 * j + tb - 1)
                else:
                    wait(pe, pt_evac, 16 * j + n - 1)
                for h in range(HPG):
                    ins = nc.tensor.transpose(ms_ps[n % 2][:, h * P:(h + 1) * P], band[:, n % 4, h, :], ident[:])
                ins.then_inc(pt_full, 1)

            def weigh_values(j, n):
                tb, hg = n // HG, n % HG
                wait(pe, pt_evac, 16 * j + n + 1)
                if n == 0:
                    wait(pe, v_evac, 4 * j + 4)
                if hg == 0:
                    wait(pe, o_norm, 4 * j + tb)
                for h in range(HPG):
                    for half in range(2):
                        col = (hg * HPG + h) * VW
                        ins = nc.tensor.matmul(o_ps[64 * half:64 * half + 64, col:col + VW],
                                               pt_sb[:, n % 2, h, 64 * half:64 * half + 64],
                                               V1[:, 2 * tb + half, hg * HPG + h, :], start=True, stop=True)
                ins.then_inc(pv_done, 1)

            def turn_attention(j, tb):
                wait(pe, o_norm, 4 * j + tb + 1)
                if tb < TB - 1:
                    wait(pe, pt_evac, 16 * j + 4 * tb + 7)
                else:
                    wait(pe, xt_evac, 2 * j + 1)
                for c in range(CC):
                    ins = nc.tensor.transpose(ms_ps[0][:, c * P:(c + 1) * P], o_sb[:, tb % 2, c * P:(c + 1) * P], ident[:])
                ins.then_inc(ot_full, 1)

            def project_attention(j, tb):
                wait(pe, ot_evac, 4 * j + tb + 1)
                if tb < TB - 1:
                    wait(pe, pt_evac, 16 * j + 4 * tb + 8)
                else:
                    wait(pe, h_gelu, 8 * j + 1)
                for c in range(CC):
                    ins = nc.tensor.matmul(ms_ps[1][:, 0:C], oT_sb[:, tb % 2, c, :], cp[:, c, :],
                                           start=(c == 0), stop=(c == CC - 1))
                ins.then_inc(cp_full, 1)

            def turn_tokens(j, half):
                wait(pe, norm_done, 8 * j + 2 * half + 2)
                if half == 0:
                    wait(pe, ot_evac, 4 * j + 3)
                else:
                    wait(pe, sum_done, 8 * j + 5)
                for n in range(2):
                    for c in range(CC):
                        ins = nc.tensor.transpose(ms_ps[half][:, (n * CC + c) * P:(n * CC + c + 1) * P],
                                                  xt[:, 2 * half + n, c * P:(c + 1) * P], ident[:])
                ins.then_inc(xt_full, 1)

            def hidden(j, n):
                if n % 4 == 0:
                    wait(pe, xt_evac, 2 * j + n // 4 + 1)
                if n == 0:
                    wait(pe, sum_done, 8 * j + 3)
                elif n == 1:
                    wait(pe, ot_evac, 4 * j + 4)
                elif n == 2:
                    wait(pe, sum_done, 8 * j + 4)
                elif n == 4:
                    wait(pe, sum_done, 8 * j + 6)
                elif n != 5:
                    wait(pe, h_gelu, 8 * j + n - 1)
                for i in range(2):
                    f = 2 * (n % 4) + i
                    for c in range(CC):
                        ins = nc.tensor.matmul(ms_ps[HIDDEN_BANK[n]][:, i * HALF:(i + 1) * HALF],
                                               w1[:, c, f * P:(f + 1) * P], x1T[:, c, :],
                                               start=(c == 0), stop=(c == CC - 1))
                ins.then_inc(h_full, 1)

            def feed_out(j, n, part, ahead):
                if part == 0:
                    wait(pe, h_gelu, 8 * j + 4 * (n // 2) + 4)
                if part == 0 and n < 2 and ahead:
                    wait(pe, g_evac, 4 * j + 9 + n)
                for f in range(part * FC // 2, (part + 1) * FC // 2):
                    ins = nc.tensor.matmul(ms_ps[FEED_BANK[n]][:, 0:C], hT[:, f, (n % 2) * P:(n % 2 + 1) * P], w2[:, f, :],
                                           start=(f == 0), stop=(f == FC - 1))
                if part:
                    ins.then_inc(f2_full, 1)

            def body(j, main, post, late, ahead):
                for step in range(W):
                    for tb in range(TB):
                        at = step - BANDS - STRIDE * tb
                        if post and 0 <= at < 4:
                            turn_band(j - 1, 4 * tb + at)
                    if main:
                        slot_logits(j, step)
                    if post and step == TURN_AT:
                        turn_logits(j - 1, MS - 1)
                    if main and step % 4 == TURN_AT and step > 4:
                        turn_logits(j, step // 4 - 1)
                    for n in range(4):
                        if post and step == VALUES[n]:
                            values(j - 1, n)
                    for tb in range(TB):
                        at = step - BANDS - STRIDE * tb
                        if post and 2 <= at < 6:
                            weigh_values(j - 1, 4 * tb + at - 2)
                        if post and step == TURN_O[tb]:
                            turn_attention(j - 1, tb)
                        if post and step == PROJECT[tb]:
                            project_attention(j - 1, tb)
                    for half in range(2):
                        if (b := due(j, step, TURN[half], post, late)) is not None:
                            turn_tokens(b, half)
                    for n in range(8):
                        if (b := due(j, step, HIDDEN[n], post, late)) is not None:
                            hidden(b, n)
                    for n in range(4):
                        for part in range(2):
                            if (b := due(j, step, FEED[n] + part, post, late)) is not None:
                                feed_out(b, n, part, ahead)
                        if ahead and step == NEXT_G[n]:
                            project_g(j + 1, G_ORDER[n])
                    if not (post or late) and step == 52:
                        pe.wait_ge(tern_done, 1)
                    if not (post or late) and step == 12:
                        pe.wait_ge(g_evac, HG)
                        pe.wait_ge(tern_sum, 2)
                        nc.tensor.matmul(o_ps[:, 0:2], ones[:], tern[:, 0:2], start=True, stop=True).then_inc(tern_tot, 1)

            for hg in G_ORDER:
                project_g(0, hg)
            pe.wait_ge(prep_done, 5)
            pe.wait_ge(loads_b, 80)
            batches(pe, body)


def kernel(**inputs):
    import numpy as np
    import concourse.bacc as bacc
    from concourse.bass_utils import run_bass_kernel_spmd

    x = np.asarray(inputs["L0_attn_x"])
    def t(name):
        return np.ascontiguousarray(np.asarray(inputs[name]).T)

    data = {
        "xT": np.ascontiguousarray(x.transpose(0, 2, 1)),
        "x_rows": np.ascontiguousarray(x),
        "w_disp": np.ascontiguousarray(inputs["L0_attn_W_disp"]),
        "w_valT": t("L0_attn_W_val"),
        "relT": t("L0_attn_rel_pos_emb"),
        "strain_wT": t("L0_attn_strain_fused_w"),
        "strain_b": np.ascontiguousarray(inputs["L0_attn_strain_fused_b"]),
        "pos_wT": t("L0_attn_pos_proj_w"),
        "bond_w": np.ascontiguousarray(inputs["L0_attn_bond_out_w"]),
        "damage_w": np.ascontiguousarray(inputs["L0_attn_damage_out_w"]),
        "damage_b": np.ascontiguousarray(inputs["L0_attn_damage_out_b"]),
        "c_projT": t("L0_attn_c_proj_w"),
        "w1T": t("L0_ffn_W1"),
        "b1": np.ascontiguousarray(np.asarray(inputs["L0_ffn_b1"]).reshape(FC, P).T),
        "w2T": t("L0_ffn_W2"),
        "b2": np.ascontiguousarray(inputs["L0_ffn_b2"]),
    }
    nc = bacc.Bacc("TRN2", target_bir_lowering=False, num_devices=1)
    arrays = {f"in_{n}": a for n, a in data.items()}
    args = [nc.dram_tensor(f"in_{n}", a.shape, mybir.dt.from_np(a.dtype), kind="ExternalInput").ap()
            for n, a in data.items()]
    result = nc.dram_tensor("out_0", (B, T, C), F32, kind="ExternalOutput").ap()
    post_ln_block(nc, *args, result)
    r = run_bass_kernel_spmd(nc, [arrays], core_ids=[0])
    return r.results[0]["out_0"]
```
